# Optimizing a Trainium2 kernel written in Bass

```python
import numpy as np
import jax
import jax.numpy as jnp

def _softmax(x, axis=-1):
    return jax.nn.softmax(x, axis=axis)

def _gelu(x):
    return jax.nn.gelu(x, approximate=True)

def _silu(x):
    return jax.nn.silu(x)

def _sigmoid(x):
    return jax.nn.sigmoid(x)

def _layernorm(x, axis=-1, eps=1e-05):
    m = jnp.mean(x, axis=axis, keepdims=True)
    v = jnp.var(x, axis=axis, keepdims=True)
    return (x - m) / jnp.sqrt(v + eps)

def _scatter_add(tgt, idx, src, axis=0):
    return tgt.at[idx].add(src)

def _segment_sum(src, seg, n):
    return jax.ops.segment_sum(src, seg, n)
kernel_name = 'mk_macaron_d2_jaxref_r8_91cf25'

def setup_inputs(seed: int=0):
    np.random.seed(seed)
    _w = jnp.asarray

    def _L0_attn_setup():
        import jax, jax.numpy as jnp
        import numpy as np
        B, S, HID = (2, 256, 128)
        H = 16
        D = HID // H
        SPARSITY = 0.9

        def _sparse_attn(x, Wq, bq, Wk, bk, Wv, bv, Wo, bo):
            b, s, hid = x.shape
            d = hid // H

            def heads(y):
                return y.reshape(b, s, H, d).transpose(0, 2, 1, 3)
            Q = heads(x @ Wq + bq)
            K = heads(x @ Wk + bk)
            V = heads(x @ Wv + bv)
            scores = jnp.einsum('bhqd,bhkd->bhqk', Q, K) / np.sqrt(d)
            k_keep = int(s * (1.0 - SPARSITY))
            vals, idx = jax.lax.top_k(scores, k_keep)
            n = b * H * s
            rows = jnp.arange(n)[:, None]
            sparse = jnp.zeros((n, s), scores.dtype).at[rows, idx.reshape(n, k_keep)].set(vals.reshape(n, k_keep)).reshape(b, H, s, s)
            attn = jax.nn.softmax(sparse, axis=-1)
            out = jnp.einsum('bhqk,bhkd->bhqd', attn, V)
            out = out.transpose(0, 2, 1, 3).reshape(b, s, hid)
            return out @ Wo + bo
        key = jax.random.key(seed)
        ks = jax.random.split(key, 5)
        sc = 1.0 / np.sqrt(HID)
        inp = {'x': jax.random.normal(ks[0], (B, S, HID), jnp.float32)}
        for i, name in enumerate(['q', 'k', 'v', 'o']):
            inp[f'W{name}'] = jax.random.normal(ks[i + 1], (HID, HID), jnp.float32) * sc
            inp[f'b{name}'] = jnp.zeros((HID,), jnp.float32)
        return inp
    _L0_attn_in = _L0_attn_setup()

    def _L0_ffn_setup():
        import jax, jax.numpy as jnp
        import numpy as np
        D_MODEL, D_FF, NUM_EXPERTS, RANK, TOP_K = (128, 512, 8, 16, 2)
        B, S = (8, 256)

        def _expert_ffn(h, wi_w, wo_w, A, Bm):
            inter = jnp.einsum('bsd,fd->bsf', h, wi_w)
            lora = jnp.einsum('bsr,fr->bsf', jnp.einsum('bsd,rd->bsr', h, A), Bm)
            inter = jax.nn.relu(inter + lora)
            return jnp.einsum('bsf,df->bsd', inter, wo_w)
        key = jax.random.key(seed)
        ks = jax.random.split(key, 8)
        hidden_states = jax.random.normal(ks[0], (B, S, D_MODEL), dtype=jnp.float32)
        wi_w = jax.random.normal(ks[1], (D_FF, D_MODEL), dtype=jnp.float32) * (1.0 / np.sqrt(D_MODEL))
        wo_w = jax.random.normal(ks[2], (D_MODEL, D_FF), dtype=jnp.float32) * (1.0 / np.sqrt(D_FF))
        lora_As = jax.random.uniform(ks[3], (NUM_EXPERTS, RANK, D_MODEL), dtype=jnp.float32, minval=-1.0, maxval=1.0) / np.sqrt(D_MODEL)
        lora_Bs = jax.random.normal(ks[4], (NUM_EXPERTS, D_FF, RANK), dtype=jnp.float32) * 0.02
        top_k_indices = jnp.arange(TOP_K, dtype=jnp.int32)
        top_k_values = jax.random.uniform(ks[5], (TOP_K,), dtype=jnp.float32)
        return {'hidden_states': hidden_states, 'wi_w': wi_w, 'wo_w': wo_w, 'lora_As': lora_As, 'lora_Bs': lora_Bs, 'top_k_indices': top_k_indices, 'top_k_values': top_k_values}
    _L0_ffn_in = _L0_ffn_setup()

    def _L1_attn_setup():
        import jax, jax.numpy as jnp
        import numpy as np
        import math
        B, T, C, NH = (4, 256, 128, 16)
        HS = C // NH

        def rope_cache(dim, max_pos):
            half = dim // 2
            inv_freq = 1.0 / 10000.0 ** (jnp.arange(half, dtype=jnp.float32) * 2.0 / dim)
            ang = jnp.arange(max_pos, dtype=jnp.float32)[:, None] * inv_freq[None, :]
            return (jnp.cos(ang), jnp.sin(ang))

        def apply_rope(x, cos, sin):
            x0 = x[..., 0::2]
            x1 = x[..., 1::2]
            c = cos[None, None, :, :]
            s = sin[None, None, :, :]
            r0 = x0 * c - x1 * s
            r1 = x0 * s + x1 * c
            return jnp.stack([r0, r1], axis=-1).reshape(x.shape)
        key = jax.random.key(seed)
        ks = jax.random.split(key, 5)
        sc = 1.0 / math.sqrt(C)
        return {'x': jax.random.normal(ks[0], (B, T, C), jnp.float32), 'Wq': jax.random.normal(ks[1], (C, C), jnp.float32) * sc, 'bq': jnp.zeros((C,), jnp.float32), 'Wk': jax.random.normal(ks[2], (C, C), jnp.float32) * sc, 'bk': jnp.zeros((C,), jnp.float32), 'Wv': jax.random.normal(ks[3], (C, C), jnp.float32) * sc, 'bv': jnp.zeros((C,), jnp.float32), 'Wp': jax.random.normal(ks[4], (C, C), jnp.float32) * sc, 'bp': jnp.zeros((C,), jnp.float32)}
    _L1_attn_in = _L1_attn_setup()

    def _L1_ffn_setup():
        import jax, jax.numpy as jnp
        import numpy as np
        EPS = 1e-05

        @jax.custom_vjp
        def ste_quantize(w):
            scale = jnp.maximum(jnp.mean(jnp.abs(w)), EPS)
            return jnp.clip(jnp.round(w / scale), -1.0, 1.0)

        def _ste_fwd(w):
            return (ste_quantize(w), None)

        def _ste_bwd(_, g):
            return (g,)
        ste_quantize.defvjp(_ste_fwd, _ste_bwd)
        key = jax.random.key(seed)
        k1, k2 = jax.random.split(key)
        x = jax.random.normal(k1, (8, 1024, 128), dtype=jnp.float32)
        weight = jax.random.normal(k2, (128, 128), dtype=jnp.float32) * 0.02
        return {'x': x, 'weight': weight}
    _L1_ffn_in = _L1_ffn_setup()
    _d = {'L0_attn_x': _L0_attn_in['x'], 'L0_attn_Wq': _L0_attn_in['Wq'], 'L0_attn_bq': _L0_attn_in['bq'], 'L0_attn_Wk': _L0_attn_in['Wk'], 'L0_attn_bk': _L0_attn_in['bk'], 'L0_attn_Wv': _L0_attn_in['Wv'], 'L0_attn_bv': _L0_attn_in['bv'], 'L0_attn_Wo': _L0_attn_in['Wo'], 'L0_attn_bo': _L0_attn_in['bo'], 'L0_ffn_wi_w': _L0_ffn_in['wi_w'], 'L0_ffn_wo_w': _L0_ffn_in['wo_w'], 'L0_ffn_lora_As': _L0_ffn_in['lora_As'], 'L0_ffn_lora_Bs': _L0_ffn_in['lora_Bs'], 'L0_ffn_top_k_indices': _L0_ffn_in['top_k_indices'], 'L0_ffn_top_k_values': _L0_ffn_in['top_k_values'], 'L1_attn_Wq': _L1_attn_in['Wq'], 'L1_attn_bq': _L1_attn_in['bq'], 'L1_attn_Wk': _L1_attn_in['Wk'], 'L1_attn_bk': _L1_attn_in['bk'], 'L1_attn_Wv': _L1_attn_in['Wv'], 'L1_attn_bv': _L1_attn_in['bv'], 'L1_attn_Wp': _L1_attn_in['Wp'], 'L1_attn_bp': _L1_attn_in['bp'], 'L1_ffn_weight': _L1_ffn_in['weight']}
    _x0 = _d['L0_attn_x']
    _d['L0_attn_x'] = jax.random.normal(jax.random.fold_in(jax.random.key(seed), 1), (2, 1024, 128), dtype=_x0.dtype)
    del _x0
    return _d

def reference(L0_attn_x, L0_attn_Wq, L0_attn_bq, L0_attn_Wk, L0_attn_bk, L0_attn_Wv, L0_attn_bv, L0_attn_Wo, L0_attn_bo, L0_ffn_wi_w, L0_ffn_wo_w, L0_ffn_lora_As, L0_ffn_lora_Bs, L0_ffn_top_k_indices, L0_ffn_top_k_values, L1_attn_Wq, L1_attn_bq, L1_attn_Wk, L1_attn_bk, L1_attn_Wv, L1_attn_bv, L1_attn_Wp, L1_attn_bp, L1_ffn_weight):

    def _L0_attn_ref(x, Wq, bq, Wk, bk, Wv, bv, Wo, bo):
        import jax, jax.numpy as jnp
        import numpy as np
        B, S, HID = (2, 256, 128)
        H = 16
        D = HID // H
        SPARSITY = 0.9

        def _sparse_attn(x, Wq, bq, Wk, bk, Wv, bv, Wo, bo):
            b, s, hid = x.shape
            d = hid // H

            def heads(y):
                return y.reshape(b, s, H, d).transpose(0, 2, 1, 3)
            Q = heads(x @ Wq + bq)
            K = heads(x @ Wk + bk)
            V = heads(x @ Wv + bv)
            scores = jnp.einsum('bhqd,bhkd->bhqk', Q, K) / np.sqrt(d)
            k_keep = int(s * (1.0 - SPARSITY))
            vals, idx = jax.lax.top_k(scores, k_keep)
            n = b * H * s
            rows = jnp.arange(n)[:, None]
            sparse = jnp.zeros((n, s), scores.dtype).at[rows, idx.reshape(n, k_keep)].set(vals.reshape(n, k_keep)).reshape(b, H, s, s)
            attn = jax.nn.softmax(sparse, axis=-1)
            out = jnp.einsum('bhqk,bhkd->bhqd', attn, V)
            out = out.transpose(0, 2, 1, 3).reshape(b, s, hid)
            return out @ Wo + bo
        return _sparse_attn(x, Wq, bq, Wk, bk, Wv, bv, Wo, bo)

    def _L0_ffn_ref(hidden_states, wi_w, wo_w, lora_As, lora_Bs, top_k_indices, top_k_values):
        import jax, jax.numpy as jnp
        import numpy as np
        D_MODEL, D_FF, NUM_EXPERTS, RANK, TOP_K = (128, 512, 8, 16, 2)
        B, S = (8, 256)

        def _expert_ffn(h, wi_w, wo_w, A, Bm):
            inter = jnp.einsum('bsd,fd->bsf', h, wi_w)
            lora = jnp.einsum('bsr,fr->bsf', jnp.einsum('bsd,rd->bsr', h, A), Bm)
            inter = jax.nn.relu(inter + lora)
            return jnp.einsum('bsf,df->bsd', inter, wo_w)
        out = jnp.zeros_like(hidden_states)
        for k in range(top_k_values.shape[0]):
            A = jnp.take(lora_As, top_k_indices[k], axis=0)
            Bm = jnp.take(lora_Bs, top_k_indices[k], axis=0)
            out = out + top_k_values[k] * _expert_ffn(hidden_states, wi_w, wo_w, A, Bm)
        return out

    def _L1_attn_ref(x, Wq, bq, Wk, bk, Wv, bv, Wp, bp):
        import jax, jax.numpy as jnp
        import numpy as np
        import math
        B, T, C, NH = (4, 256, 128, 16)
        HS = C // NH

        def rope_cache(dim, max_pos):
            half = dim // 2
            inv_freq = 1.0 / 10000.0 ** (jnp.arange(half, dtype=jnp.float32) * 2.0 / dim)
            ang = jnp.arange(max_pos, dtype=jnp.float32)[:, None] * inv_freq[None, :]
            return (jnp.cos(ang), jnp.sin(ang))

        def apply_rope(x, cos, sin):
            x0 = x[..., 0::2]
            x1 = x[..., 1::2]
            c = cos[None, None, :, :]
            s = sin[None, None, :, :]
            r0 = x0 * c - x1 * s
            r1 = x0 * s + x1 * c
            return jnp.stack([r0, r1], axis=-1).reshape(x.shape)
        Bx, Tx, Cx = x.shape

        def split_heads(y):
            return y.reshape(Bx, Tx, NH, HS).transpose(0, 2, 1, 3)
        q = split_heads(x @ Wq + bq)
        k = split_heads(x @ Wk + bk)
        v = split_heads(x @ Wv + bv)
        cos, sin = rope_cache(HS, Tx)
        q = apply_rope(q, cos, sin)
        k = apply_rope(k, cos, sin)
        att = jnp.einsum('bhqd,bhkd->bhqk', q, k) * (1.0 / math.sqrt(HS))
        causal = jnp.tril(jnp.ones((Tx, Tx), bool))
        att = jnp.where(causal[None, None, :, :], att, jnp.float32(-10000000000.0))
        att = jax.nn.softmax(att, axis=-1)
        y = jnp.einsum('bhqk,bhkd->bhqd', att, v)
        y = y.transpose(0, 2, 1, 3).reshape(Bx, Tx, Cx)
        return y @ Wp + bp

    def _L1_ffn_ref(x, weight):
        import jax, jax.numpy as jnp
        import numpy as np
        EPS = 1e-05

        @jax.custom_vjp
        def ste_quantize(w):
            scale = jnp.maximum(jnp.mean(jnp.abs(w)), EPS)
            return jnp.clip(jnp.round(w / scale), -1.0, 1.0)

        def _ste_fwd(w):
            return (ste_quantize(w), None)

        def _ste_bwd(_, g):
            return (g,)
        ste_quantize.defvjp(_ste_fwd, _ste_bwd)
        w_ternary = ste_quantize(weight)
        scale = jnp.maximum(jnp.mean(jnp.abs(weight)), EPS)
        return jnp.einsum('bsi,oi->bso', x, w_ternary * scale)
    x = L0_attn_x
    x = x + 0.5 * _L0_ffn_ref(_layernorm(x, axis=-1), L0_ffn_wi_w, L0_ffn_wo_w, L0_ffn_lora_As, L0_ffn_lora_Bs, L0_ffn_top_k_indices, L0_ffn_top_k_values)
    x = x + _L0_attn_ref(_layernorm(x, axis=-1), L0_attn_Wq, L0_attn_bq, L0_attn_Wk, L0_attn_bk, L0_attn_Wv, L0_attn_bv, L0_attn_Wo, L0_attn_bo)
    x = x + 0.5 * _L0_ffn_ref(_layernorm(x, axis=-1), L0_ffn_wi_w, L0_ffn_wo_w, L0_ffn_lora_As, L0_ffn_lora_Bs, L0_ffn_top_k_indices, L0_ffn_top_k_values)
    x = x + 0.5 * _L1_ffn_ref(_layernorm(x, axis=-1), L1_ffn_weight)
    x = x + _L1_attn_ref(_layernorm(x, axis=-1), L1_attn_Wq, L1_attn_bq, L1_attn_Wk, L1_attn_bk, L1_attn_Wv, L1_attn_bv, L1_attn_Wp, L1_attn_bp)
    x = x + 0.5 * _L1_ffn_ref(_layernorm(x, axis=-1), L1_ffn_weight)
    return x

_drawn_inputs = setup_inputs


def setup_inputs(seed=0):
    import zlib

    import numpy as np

    out = dict(_drawn_inputs(seed))
    spreads = {'L0_attn_bq': (0.0, 2.0),
     'L0_attn_bk': (0.0, 2.0),
     'L0_attn_bv': (0.0, 0.488),
     'L0_attn_bo': (0.0, 0.475),
     'L1_attn_bq': (0.0, 2.0),
     'L1_attn_bk': (0.0, 2.0),
     'L1_attn_bv': (0.0, 0.553),
     'L1_attn_bp': (0.0, 0.565)}
    factors = {'L0_ffn_lora_As': 2.983,
     'L0_ffn_lora_Bs': 2.999,
     'L0_ffn_top_k_values': 8.0,
     'L0_attn_Wq': 4.1,
     'L0_attn_Wk': 2.97,
     'L1_attn_Wq': 4.695,
     'L1_attn_Wk': 4.319,
     'L1_ffn_weight': 2.878}
    for name, (base, spread) in spreads.items():
        noise = np.random.default_rng([zlib.crc32(name.encode()), seed]).standard_normal(out[name].shape)
        drawn = base * np.exp(spread * noise) if base else spread * noise
        out[name] = jnp.asarray(drawn.astype(out[name].dtype))
    for name, factor in factors.items():
        out[name] = (out[name] * factor).astype(out[name].dtype)
    return out
```

```python
import numpy as np
from contextlib import ExitStack, contextmanager

import concourse.bass as bass
from concourse import mybir

P = 128
BATCH, SEQ, HID = 2, 1024, 128
HEADS, HD = 16, 8
TILES = BATCH * SEQ // P
QT_TILES = SEQ // P
HB = BATCH * HEADS
FF, EXPERTS, RANK, TOPK = 512, 8, 16, 2
FC = FF // P
KEEP = int(SEQ * (1.0 - 0.9))
EPS = 1e-5
BIG = 2.0 ** 100
LOWEST = -3.0e38
CROWS = 9 * HD
ZROWS, YROWS = CROWS + 3, CROWS + 6
Z_START = 1.29
AIM1, AIM2 = 92.5, 90.5
DENSITY1, DENSITY2 = 190.0, 225.0
NSORT = 24
SEGS = 8
ISQ = float(1.0 / np.sqrt(np.float32(HD)))

C_ID, C_UP, C_HEAD, C_MASK = 0, 128, 256, 384
C_HSEL = C_MASK + 896
C_EXP = C_HSEL + HEADS
C_SEL0 = C_EXP + 1
C_SEL1 = C_SEL0 + 18
C_IOTA = C_SEL1 + 9
C_ROPE = C_IOTA + NSORT + 1
C_ALL = C_ROPE + 2 * SEQ


def shape_constants():
    c = np.zeros((P, C_ALL), np.float32)
    r = np.arange(P)
    c[:, C_ID:C_ID + P] = np.eye(P)
    c[:, C_UP:C_UP + P] = r[None, :] > r[:, None]
    c[:, C_HEAD:C_HEAD + P] = (r[:, None] // HD == r[None, :] // HD) / SEQ
    c[:, C_MASK:C_MASK + 896] = r[:, None] > np.arange(896)[None, :] - 384
    c[:, C_HSEL:C_HSEL + HEADS] = (r[:, None] // HD == np.arange(HEADS)[None, :]) / SEQ
    c[:, C_EXP] = r // RANK
    for d in range(HD + 1):
        for quad in (0, 1):
            c[32 * quad + d, C_SEL0 + d] = 1
        for quad in (2, 3):
            for part in range(3 if d < HD else 1):
                row = part * HD + d if d < HD else 3 * HD
                c[32 * quad + row, C_SEL0 + 9 + d] = 1
        for quad in range(4):
            c[32 * quad + d, C_SEL1 + d] = 1
    c[:, C_IOTA:C_IOTA + NSORT + 1] = np.arange(NSORT + 1)
    half = HD // 2
    inv = (1.0 / np.float32(10000.0) ** (np.arange(half, dtype=np.float32) * np.float32(2.0) / np.float32(HD))).astype(np.float32)
    ang = np.arange(SEQ, dtype=np.float32)[:, None] * inv[None, :]
    freq = (r % HD) // 2
    c[:, C_ROPE:C_ROPE + SEQ] = np.cos(ang).T[freq]
    c[:, C_ROPE + SEQ:] = np.sin(ang).T[freq] * np.where(r % 2 == 0, -1.0, 1.0)[:, None]
    return c


def macaron_kernel(nc, consts, x_in, wq0, wk0, wv0, wo0, rows0, cols0, wi, wo_ff, lora_a, lora_b, idx, val,
                   wq1, wk1, wv1, wo1, rows1, cols1, wq1s, wk1s, wt, qs, ks, out):
    f32, bf, i32 = mybir.dt.float32, mybir.dt.bfloat16, mybir.dt.int32
    ALU, ACT, AX = mybir.AluOpType, mybir.ActivationFunctionType, mybir.AxisListType
    ctx = ExitStack()
    with ctx:
        def sb(name, shape, dt=f32):
            return ctx.enter_context(nc.sbuf_tensor(name, shape, dt))

        def sem(name):
            return ctx.enter_context(nc.semaphore(name))

        x = sb("x", [P, TILES, HID])
        ao = sb("ao", [P, TILES, HID])
        cst = sb("cst", [P, C_ALL])
        ident = cst[:, C_ID:C_ID + P]
        identb = sb("identb", [P, P], bf)
        negbig = sb("negbig", [P, P], bf)
        upb = sb("upb", [P, P], bf)
        maskb = sb("maskb", [P, 896], bf)
        ones = sb("ones", [P, P])
        w0 = sb("w0", [P, 3, P]); w1 = sb("w1", [P, 3, P])
        w1s = sb("w1s", [P, 2, P])
        wo_a = sb("wo_a", [P, 2, P])
        brow = sb("brow", [1, 2, 4, P])
        bcol = sb("bcol", [P, 8])
        la = sb("la", [P, P]); lb = sb("lb", [P, FF]); lbs = sb("lbs", [P, TOPK, FF])
        wi_sb = sb("wi_sb", [P, FF]); wo_sb = sb("wo_sb", [P, FC, P])
        idx_sb = sb("idx_sb", [P, TOPK], i32); idxf = sb("idxf", [P, TOPK]); esel = sb("esel", [P, TOPK])
        val_sb = sb("val_sb", [P, TOPK])
        wk_ff = sb("wk_ff", [P, TOPK, FF])
        wt_sb = sb("wt_sb", [P, P]); wtern = sb("wtern", [P, P]); wneg = sb("wneg", [P, P])
        wabs = sb("wabs", [P, 1]); wscale = sb("wscale", [P, 3])
        stat = sb("stat", [P, TILES, 6]); ln = sb("ln", [P, 6, TILES])
        eps = sb("eps", [P, 1])
        h = sb("h", [P, 2, 4, P]); hT = sb("hT", [P, 2, 4 * P])
        relu0 = sb("relu0", [P, 2, 4 * P]); relu1 = sb("relu1", [P, 2, 4 * P]); mix = sb("mix", [P, FC, 4 * P])
        qk_t = sb("qk_t", [P, 2, 4 * P]); res1 = sb("res1", [P, 2, 4 * P])
        rot = sb("rot", [P, 2, 4 * P])
        parts = sb("parts", [P, 2, 3, 4 * P], bf)
        qb = sb("qb", [P, TILES, HID], bf)
        qtok = sb("qtok", [P, TILES, HID], bf)
        kf = sb("kf", [P, 4, P])
        vf = sb("vf", [P, TILES, HID]); vres = sb("vres", [P, TILES, HID])
        vp = sb("vp", [P, 3, TILES, HID], bf)
        krow = sb("krow", [1, 2, P]); kcol = sb("kcol", [P, 1]); cov = sb("cov", [P, 144], bf)
        qc = sb("qc", [P, HID])
        mu = sb("mu", [P, TILES, HEADS]); sd = sb("sd", [P, TILES, HEADS]); par = sb("par", [P, 5, TILES, HEADS])
        QT = sb("QT", [P, 4, SEQ], bf); KT = sb("KT", [P, 4, SEQ], bf)
        pst = sb("pst", [P, 2, 5, QT_TILES])
        vg = sb("vg", [P, 2, QT_TILES, 32]); vu = sb("vu", [P, 2, QT_TILES, 32], bf)
        rmax = sb("rmax", [P, 2, QT_TILES]); cs = sb("cs", [P, 2, 2])
        t1 = sb("t1", [P, 2]); off2 = sb("off2", [P, 2]); cnt = sb("cnt", [P, QT_TILES])
        junk = sb("junk", [P, SEQ], bf); ind = sb("ind", [P, 2, SEQ], bf)
        cand = sb("cand", [P, QT_TILES, SEGS * 8]); cand2 = sb("cand2", [P, 2, SEGS * 8])
        srt = sb("srt", [P, QT_TILES, NSORT + 1])
        sel = sb("sel", [P, QT_TILES, NSORT + 1]); sm = sb("sm", [P, 12, QT_TILES])
        tm = sb("tm", [P, QT_TILES, 2]); tmr = sb("tmr", [P, 2, QT_TILES, 2])
        tmp = sb("tmp", [P, QT_TILES, 2, 3], bf); tmT = sb("tmT", [48, P], bf)
        em = sb("em", [P, 2, QT_TILES]); badt = sb("badt", [P, QT_TILES + 1]); badi = sb("badi", [1, QT_TILES + 1], i32)
        nb = sb("nb", [P, 2, 512], bf); G = sb("G", [P, 2, 512]); osb = sb("osb", [P, 512])
        fin = sb("fin", [P, 2, QT_TILES, 9]); frec = sb("frec", [P, QT_TILES])
        mark = sb("mark", [1, 2])
        fw = sb("fw", [P, SEQ]); fm = sb("fm", [P, 8])
        ps = ctx.enter_context(nc.psum_tensor("ps", [P, 8, 512], f32))

        const_in = sem("const_in")
        x_in_done = sem("x_in_done")
        out_done = sem("out_done")
        passed = sem("passed")
        dve_seq = sem("dve_seq")
        pool_seq = sem("pool_seq")
        prep_done = sem("prep_done")
        ffw_psum = sem("ffw_psum")
        ffw_done = sem("ffw_done")
        tern_psum = sem("tern_psum")
        tern_done = sem("tern_done")
        var_ready = sem("var_ready")
        sd_ready = sem("sd_ready")
        h_ready = sem("h_ready")
        hT_psum = sem("hT_psum")
        hT_ready = sem("hT_ready")
        a_psum = sem("a_psum")
        relu0_ready = sem("relu0_ready")
        relu1_ready = sem("relu1_ready")
        mix_ready = sem("mix_ready")
        y_psum = sem("y_psum")
        x_ready = sem("x_ready")
        qk_psum = sem("qk_psum")
        qk_read = sem("qk_read")
        part_ready = sem("part_ready")
        part_stored = sem("part_stored")
        tok_psum = sem("tok_psum")
        tok_read = sem("tok_read")
        kf_ready = sem("kf_ready")
        kf_used = sem("kf_used")
        cov_psum = sem("cov_psum")
        cov_row = sem("cov_row")
        cov_full = sem("cov_full")
        cov_ready = sem("cov_ready")
        qb_ready = sem("qb_ready")
        stat_psum = sem("stat_psum")
        stat_read = sem("stat_read")
        sd2_var = sem("sd2_var")
        sd2_ready = sem("sd2_ready")
        par_ready = sem("par_ready")
        qk_loaded0 = sem("qk_loaded0")
        qk_loaded1 = sem("qk_loaded1")
        staged = sem("staged")
        s_ready = sem("s_ready")
        rmax_done = sem("rmax_done")
        c0_done = sem("c0_done")
        t1_ready = sem("t1_ready")
        c1_done = sem("c1_done")
        t2_ready = sem("t2_ready")
        ind_ready = sem("ind_ready")
        masked = sem("masked")
        bad_ready = sem("bad_ready")
        bad_psum = sem("bad_psum")
        bad_int = sem("bad_int")
        fb_s = sem("fb_s")
        fb_read = sem("fb_read")
        tm_ready = sem("tm_ready")
        tm_psum = sem("tm_psum")
        tm_copied = sem("tm_copied")
        tm_loaded = sem("tm_loaded")
        mx_ready = sem("mx_ready")
        em_ready = sem("em_ready")
        pst_ready = sem("pst_ready")
        v_ready = sem("v_ready")
        s_free = sem("s_free")
        z_ready = sem("z_ready")
        n_ready = sem("n_ready")
        l_ready = sem("l_ready")
        exp_ready = sem("exp_ready")
        pv_done = sem("pv_done")
        o_copied = sem("o_copied")
        fin_psum = sem("fin_psum")
        fin_done = sem("fin_done")

        HT_READY_0 = 2
        RELU0_READY_0 = 2
        RELU1_READY_0 = 2
        MIX_READY_0 = 2
        Y_PSUM_0 = 1
        X_READY_0 = 2
        QK_READ_0 = 2
        PART_STORED_0 = 32
        TOK_READ_0 = 2
        KF_USED_0 = 1
        STAT_READ_0 = 2
        L_READY_0 = 33
        S_FREE_0 = 2
        N_READY_0 = 1
        EXP_READY_0 = 1
        PV_DONE_0 = 18
        FB_READ_0 = 1
        O_COPIED_0 = 1
        FIN_PSUM_0 = 1
        FIN_DONE_0 = 1
        TM_LOADED_0 = 128
        BAD_READY_0 = 1

        def settled(eng):
            eng.sem_inc(passed, 1)

        class Seq:
            def __init__(self, eng, counter):
                self.eng, self.s, self.n, self.k = eng, counter, 0, 0

            def link(self, ins, plain=False):
                self.n, self.k = self.n + 1, self.k + 1
                ins.then_inc(self.s, 1)
                self.eng.wait_ge(self.s, self.n)
                if plain:
                    settled(self.eng)

            @contextmanager
            def loop(self, count, per):
                start, k = self.n, self.k
                with self.eng.Fori(0, count) as i:
                    self.n = start + i * per
                    yield i
                assert self.k - k == per, (self.k - k, per)
                self.n, self.k = start + count * per, k + per * count

        HALVES0 = [(q, k) for q in range(2) for k in range(8)]
        HALVES1 = [(q, k) for q in range(2) for k in range(4 * q + 4)]
        SCHED0 = [[], [0, 1], [2, 3], [4, 5], [6, 7], [8, 9], [10, 11, 12], [13, 14, 15]]
        SCHED1 = [[], [0, 1], [2, 3], [4, 5], [6, 7], [8, 9], [10], [11]]
        halves = {0: HALVES0, 1: HALVES1}
        sched = {0: SCHED0, 1: SCHED1}
        N2 = [HB * 16, HB * 12]
        base_n = [0, HB * QT_TILES]
        base_n2 = [0, HB * 16]

        def cn(layer, hb, i):
            return base_n[layer] + hb * QT_TILES + i

        def cn2(layer, hb, c):
            return base_n2[layer] + hb * len(halves[layer]) + c

        def ch(layer, hb):
            return layer * HB + hb

        def over_heads(eng, layer, step):
            step(0, 0, None)
            with eng.Fori(0, (HB - 2) // 2) as i:
                step(i * 2 + 1, 1, i * 2)
                step(i * 2 + 2, 0, i * 2 + 1)
            step(HB - 1, 1, HB - 2)
            step(None, 0, HB - 1)

        def loaded(eng, layer, hb, p):
            if not (isinstance(hb, int) and hb < 0):
                eng.wait_ge((qk_loaded0, qk_loaded1)[p], 288 * (layer * HB // 2 + (hb - p) // 2 + 1))

        def bank(i):
            return ps[:, i, :]

        def SA(i):
            return ps[:, 2 * (i % 2):2 * (i % 2) + 2, :].rearrange("p a b -> p (a b)")

        ZB, LB, OB, XB = 4, 5, 6, 7

        block = ctx.enter_context(nc.Block())

        @block.sync
        def _(sp):
            sp.dma_start(x[:], x_in.rearrange("(t p) d -> p t d", p=P)).then_inc(x_in_done, 16)
            for dst, src in ((cst[:], consts), (la[:], lora_a), (lb[:], lora_b), (wi_sb[:], wi),
                             (wo_sb[:], wo_ff), (idx_sb[:], idx), (val_sb[:], val), (wt_sb[:], wt),
                             (w0[:, 0, :], wq0), (w0[:, 1, :], wk0), (w0[:, 2, :], wv0), (wo_a[:, 0, :], wo0),
                             (w1[:, 0, :], wq1), (w1[:, 1, :], wk1), (w1[:, 2, :], wv1), (wo_a[:, 1, :], wo1),
                             (w1s[:, 0, :], wq1s), (w1s[:, 1, :], wk1s),
                             (brow[0:1, 0, :, :], rows0), (brow[0:1, 1, :, :], rows1),
                             (bcol[:, 0:2], cols0), (bcol[:, 2:6], cols1)):
                sp.dma_start(dst, src).then_inc(const_in, 16)

            sp.wait_ge(prep_done, 1)
            for layer in range(2):
                with sp.Fori(0, 2) as b:
                    for half in range(2):
                        kg = layer * 4 + b * 2 + half
                        sp.wait_ge(part_ready, 2 * (kg + 1))
                        for w, scr in ((0, qs), (1, ks)):
                            sp.dma_start(scr[b, :, :, half * 512:(half + 1) * 512].rearrange("a f t -> f a t"),
                                         parts[:, w, :, :]).then_inc(part_stored, 16)
                sp.wait_ge(part_stored, PART_STORED_0 + 32 * (layer * 4 + 4))

                def load(hb, p):
                    slot = ch(layer, hb) % 4
                    for i in range(3):
                        for j in range(3):
                            for dst, scr, part in ((QT, qs, i), (KT, ks, j)):
                                r0 = HD * (3 * i + j)
                                sp.dma_start(dst[r0:r0 + HD, slot, :],
                                             scr[hb // HEADS, part, bass.ds((hb % HEADS) * HD, HD), :]
                                             ).then_inc((qk_loaded0, qk_loaded1)[p], 16)

                load(0, 0)

                def step(hA, p, hB):
                    if hA is None:
                        return
                    if not (isinstance(hA, int) and hA == HB - 1):
                        sp.wait_ge(l_ready, L_READY_0 + cn2(layer, hA - 2, 0))
                        loaded(sp, layer, hA - 1, 1 - p)
                        load(hA + 1, 1 - p)
                    sp.wait_ge(tm_copied, ch(layer, hA) + 1)
                    for t in range(QT_TILES):
                        sp.dma_start(QT[CROWS:YROWS, ch(layer, hA) % 4, t * P:(t + 1) * P],
                                     tmT[6 * t:6 * t + 6, :]).then_inc(tm_loaded, 16)

                over_heads(sp, layer, step)

            sp.wait_ge(x_ready, X_READY_0 + 4 * 6)
            sp.dma_start(out.rearrange("(t p) d -> p t d", p=P), x[:]).then_inc(out_done, 16)
            sp.wait_ge(out_done, 16)

        STAGES = [("ffn", 0, 0), ("qkv", 0, None), ("proj", 0, 1), ("ffn", 1, 2),
                  ("tern", 0, 3), ("qkv", 1, None), ("proj", 1, 4), ("tern", 1, 5)]
        LN_OF = {0: 0, 1: 1, 3: 2, 4: 3, 5: 4, 7: 5}
        X_BEFORE = {0: 0, 1: 1, 3: 2, 4: 3, 5: 4, 7: 5}

        def groups(eng, seq, per, body):
            if seq is None:
                with eng.Fori(0, 2) as b:
                    for half in range(2):
                        body(b, half)
            else:
                with seq.loop(2, per) as b:
                    for half in range(2):
                        body(b, half)

        def attention_of(s):
            return {1: 0, 5: 1}.get(s)

        @block.gpsimd
        def _(pool):
            for counter, start in (
                    (hT_ready, HT_READY_0), (relu0_ready, RELU0_READY_0), (relu1_ready, RELU1_READY_0), (mix_ready, MIX_READY_0),
                    (y_psum, Y_PSUM_0), (x_ready, X_READY_0), (qk_read, QK_READ_0), (part_stored, PART_STORED_0),
                    (tok_read, TOK_READ_0), (kf_used, KF_USED_0), (stat_read, STAT_READ_0), (l_ready, L_READY_0),
                    (s_free, S_FREE_0), (n_ready, N_READY_0), (exp_ready, EXP_READY_0), (pv_done, PV_DONE_0),
                    (fb_read, FB_READ_0), (o_copied, O_COPIED_0), (fin_psum, FIN_PSUM_0), (fin_done, FIN_DONE_0),
                    (tm_loaded, TM_LOADED_0), (bad_ready, BAD_READY_0),
            ):
                pool.sem_inc(counter, start)
            pool.wait_ge(prep_done, 1)
            for layer in range(2):
                if layer == 0:
                    pool.wait_ge(par_ready, 1)
                pool.wait_ge(v_ready, layer + 1)

                def step(hA, p, hB):
                    if hA is None:
                        return
                    b, hd = hA // HEADS, hA % HEADS
                    tl = bass.ds(b * QT_TILES, QT_TILES)
                    if layer == 0:
                        for k in range(5):
                            ins = nc.gpsimd.tensor_copy(pst[:, p, k, :].rearrange("p (t a) -> p t a", a=1),
                                                        par[:, k, tl, bass.ds(hd, 1)])
                        ins.then_inc(pst_ready, 1)
                    pool.wait_ge(pv_done, PV_DONE_0 + cn2(layer, hA - 1, 0))
                    nc.gpsimd.tensor_copy(vg[:, p, :, 0:HD], vf[:, tl, bass.ds(hd * HD, HD)]).then_inc(staged, 1)
                    if layer == 0:
                        for part in range(3):
                            nc.gpsimd.tensor_copy(vu[:, p, :, part * HD:(part + 1) * HD],
                                                  vp[:, part, tl, bass.ds(hd * HD, HD)]).then_inc(staged, 1)
                        for i in range(QT_TILES):
                            pool.wait_ge(c0_done, hA * QT_TILES + i + 1)
                            settled(pool)
                            nc.gpsimd.tensor_scalar(t1[:, i % 2:i % 2 + 1], cs[:, 0, i % 2:i % 2 + 1], pst[:, p, 1, i:i + 1],
                                                    pst[:, p, 2, i:i + 1], ALU.mult, ALU.add).then_inc(t1_ready, 1)
                            nc.gpsimd.tensor_scalar(off2[:, i % 2:i % 2 + 1], cs[:, 0, i % 2:i % 2 + 1], pst[:, p, 1, i:i + 1],
                                                    pst[:, p, 3, i:i + 1], ALU.mult, ALU.add).then_inc(pool_seq, 1)
                            pool.wait_ge(pool_seq, hA * QT_TILES + i + 1)
                            pool.wait_ge(c1_done, hA * QT_TILES + i + 1)
                            pool.wait_ge(bad_ready, BAD_READY_0 + hA)
                            settled(pool)
                            nc.gpsimd.tensor_scalar(srt[:, i, 0:1], cs[:, 1, i % 2:i % 2 + 1], pst[:, p, 4, i:i + 1],
                                                    off2[:, i % 2:i % 2 + 1], ALU.mult, ALU.add).then_inc(t2_ready, 1)

                over_heads(pool, layer, step)

        @block.scalar
        def _(act):
            def layer_norm(s):
                n = LN_OF[s]
                act.wait_ge(var_ready, n + 1)
                nc.scalar.activation(ln[:, 2, :], ln[:, 1, :], ACT.Sqrt, bias=eps[:]).then_inc(sd_ready, 1)

            def stage(s):
                kind, c, xo = STAGES[s]

                def body(b, half):
                    g = b * 2 + half
                    gg = 4 * s + g
                    act.wait_ge(hT_psum, gg + 1)
                    nc.scalar.activation(hT[:, half, :], bank(XB), ACT.Copy).then_inc(hT_ready, 1)
                    if kind == "ffn":
                        for fc in range(FC):
                            u = (c * 4 + g) * FC + fc
                            act.wait_ge(a_psum, 2 * u + 1)
                            act.wait_ge(mix_ready, MIX_READY_0 + u - 1)
                            nc.scalar.activation(relu0[:, fc % 2, :], bank(fc % 2), ACT.Relu).then_inc(relu0_ready, 1)
                    if kind == "qkv":
                        kg = c * 4 + g
                        for t in range(4):
                            act.wait_ge(tok_psum, kg * 4 + t + 1)
                            tile = bass.ds(g * 4 + t, 1)
                            bk = bank(4 + t % 2)
                            if c == 0:
                                nc.scalar.activation(qtok[:, tile, :], bk[:, 0:P].rearrange("p (a d) -> p a d", a=1),
                                                     ACT.Copy, scale=ISQ)
                                if t == 0:
                                    act.wait_ge(kf_used, KF_USED_0 + g)
                                nc.scalar.activation(kf[:, t, :], bk[:, P:2 * P], ACT.Copy).then_inc(kf_ready, 1)
                            nc.scalar.activation(vf[:, tile, :], bk[:, 2 * P:3 * P].rearrange("p (a d) -> p a d", a=1),
                                                 ACT.Copy).then_inc(tok_read, 1)

                groups(act, None, 0, body)
                if kind == "qkv" and c == 0:
                    act.wait_ge(sd2_var, 1)
                    nc.scalar.activation(sd[:], sd[:], ACT.Sqrt).then_inc(sd2_ready, 1)

            def attention(layer):
                def exps(hB, cs_):
                    for c in cs_:
                        n2 = cn2(layer, hB, c)
                        act.wait_ge(l_ready, L_READY_0 + n2 + 1)
                        act.wait_ge(pv_done, PV_DONE_0 + n2 - 1)
                        nc.scalar.activation(G[:, c % 2, :], bank(LB), ACT.Exp).then_inc(exp_ready, 1)
                        if c == len0:
                            copy_o(hB, 0)

                def copy_o(hB, qb):
                    k = 2 * ch(layer, hB) + qb
                    act.wait_ge(pv_done, PV_DONE_0 + cn2(layer, hB, len(halves[layer]) if qb else len0))
                    act.wait_ge(fin_psum, FIN_PSUM_0 + k)
                    nc.scalar.activation(osb[:], bank(OB), ACT.Copy).then_inc(o_copied, 1)

                len0 = sum(1 for q, k in halves[layer] if q == 0)

                def step(hA, p, hB):
                    pB = 1 - p
                    if layer == 0 and hA is not None:
                        act.wait_ge(pst_ready, hA + 1)
                    if hB is not None and layer == 0:
                        act.wait_ge(mx_ready, hB + 1)
                        nc.scalar.activation(em[:, pB, :], sm[:, 6 + pB, :], ACT.Exp, scale=-1.0).then_inc(em_ready, 1)
                    for i in range(QT_TILES):
                        cs_ = sched[layer][i] if hB is not None else []
                        if layer == 0 and hA is not None:
                            n = hA * QT_TILES + i
                            act.wait_ge(rmax_done, n + 1)
                            nc.scalar.activation(junk[:], SA(i), ACT.Sign, bias=pst[:, p, 0, i:i + 1], scale=-1.0,
                                                 accum_out=cs[:, 0, i % 2:i % 2 + 1]).then_inc(c0_done, 1)
                        exps(hB, cs_[:1])
                        if layer == 0 and hA is not None:
                            act.wait_ge(t1_ready, n + 1)
                            act.wait_ge(c0_done, n + 1)
                            nc.scalar.activation(junk[:], SA(i), ACT.Sign, bias=t1[:, i % 2:i % 2 + 1], scale=-1.0,
                                                 accum_out=cs[:, 1, i % 2:i % 2 + 1]).then_inc(c1_done, 1)
                        exps(hB, cs_[1:])
                    if hA is not None:
                        act.wait_ge(tm_psum, ch(layer, hA) + 1)
                        act.wait_ge(tm_loaded, TM_LOADED_0 + 128 * ch(layer, hA))
                        nc.scalar.activation(tmT[:], bank(LB)[0:48, 0:64].bitcast(bf), ACT.Copy).then_inc(tm_copied, 1)
                    if hB is not None:
                        copy_o(hB, 1)

                over_heads(act, layer, step)

            act.wait_ge(const_in, 16 * 22)
            for s in range(len(STAGES)):
                if s in LN_OF:
                    layer_norm(s)
                stage(s)
                if attention_of(s) is not None:
                    attention(attention_of(s))

        @block.tensor
        def _(pe):
            mm = nc.tensor.matmul

            def stage(s):
                kind, c, xo = STAGES[s]

                def body(b, half):
                    g = b * 2 + half
                    gg = 4 * s + g
                    pe.wait_ge(h_ready, gg + 1)
                    pe.wait_ge(hT_ready, HT_READY_0 + gg)
                    for t in range(4):
                        ins = nc.tensor.transpose(bank(XB)[:, t * P:(t + 1) * P], h[:, half, t, :], ident)
                    ins.then_inc(hT_psum, 1)
                    pe.wait_ge(hT_ready, HT_READY_0 + gg + 1)
                    rhs = hT[:, half, :]
                    if xo is not None:
                        yy = 4 * xo + g
                        Y = bank(4 + half)
                        pe.wait_ge(x_ready, X_READY_0 + yy - 1)
                    if kind == "ffn":
                        def down(fc):
                            pe.wait_ge(mix_ready, MIX_READY_0 + (c * 4 + g) * FC + fc + 1)
                            for t in range(4):
                                ins = mm(Y[:, t * P:(t + 1) * P], mix[:, fc, t * P:(t + 1) * P], wo_sb[:, fc, :],
                                         start=(fc == 0 and t == 0), stop=(fc == FC - 1), skip_group_check=True)
                            return ins
                        for fc in range(FC):
                            u = (c * 4 + g) * FC + fc
                            for k in range(TOPK):
                                pe.wait_ge((relu0_ready, relu1_ready)[k], RELU0_READY_0 + u - 1)
                                ins = mm(bank(2 * k + fc % 2), wk_ff[:, k, fc * P:(fc + 1) * P], rhs, start=True, stop=True)
                                ins.then_inc(a_psum, 1)
                            if fc:
                                down(fc - 1)
                        down(FC - 1).then_inc(y_psum, 1)
                    if kind == "tern":
                        for t in range(4):
                            ins = mm(Y[:, t * P:(t + 1) * P], hT[:, half, t * P:(t + 1) * P], wtern[:], start=True, stop=True)
                        ins.then_inc(y_psum, 1)
                    if kind == "proj":
                        for t in range(4):
                            mm(Y[:, t * P:(t + 1) * P], ones[0:1, :], brow[0:1, c, 3, :], start=True, stop=False)
                            ins = mm(Y[:, t * P:(t + 1) * P], hT[:, half, t * P:(t + 1) * P], wo_a[:, c, :], start=False, stop=True)
                        ins.then_inc(y_psum, 1)
                    if kind == "qkv":
                        kg = c * 4 + g
                        w = w1 if c else w0
                        for j in range(2):
                            pe.wait_ge(qk_read, QK_READ_0 + 2 * kg + j - 1)
                            ins = mm(bank(j), w[:, j, :], rhs, start=True, stop=True)
                            if c:
                                ins = mm(bank(2 + j), w1s[:, j, :], rhs, start=True, stop=True)
                            ins.then_inc(qk_psum, 1)
                        for t in range(4):
                            pe.wait_ge(tok_read, TOK_READ_0 + kg * 4 + t - 1)
                            lo = 2 if c else 0
                            o = bank(4 + t % 2)[:, lo * P:3 * P]
                            mm(o, ones[0:1, :], brow[0:1, c, lo:3, :], start=True, stop=False)
                            mm(o, hT[:, half, t * P:(t + 1) * P], w[:, lo:3, :], start=False, stop=True).then_inc(tok_psum, 1)
                        if c == 0:
                            pe.wait_ge(kf_ready, 4 * (g + 1))
                            if half == 0:
                                pe.wait_ge(stat_read, STAT_READ_0 + b * QT_TILES)
                            for t in range(4):
                                st, sp_ = half == 0 and t == 0, half == 1 and t == 3
                                mm(bank(6)[:, 0:P], kf[:, t, :], kf[:, t, :], start=st, stop=False, skip_group_check=True)
                                mm(bank(2)[0:1, 0:P], ones[:, 0:1], kf[:, t, :], start=st, stop=sp_)
                                ins = mm(bank(3)[:, 0:1], kf[:, t, :], ones[:, 0:1], start=st, stop=sp_)
                            ins.then_inc(kf_used, 1)
                            if half == 1:
                                pe.wait_ge(cov_row, b + 1)
                                mm(bank(6)[:, 0:P], krow[0:1, 1, :], krow[0:1, 0, :], start=False, stop=True,
                                   skip_group_check=True).then_inc(cov_full, 1)
                                pe.wait_ge(cov_ready, b + 1)
                                pe.wait_ge(qb_ready, 2 * b + 2)
                                for t in range(QT_TILES):
                                    j = b * QT_TILES + t
                                    pe.wait_ge(stat_read, STAT_READ_0 + j - 1)
                                    nc.tensor.matmul(bank(2 + t % 2)[:, 0:144], qb[:, j, :], cov[:],
                                                     start=True, stop=True).then_inc(stat_psum, 1)

                groups(pe, None, 0, body)

            def attention(layer):
                nh = len(halves[layer])

                def product(hB, p, c):
                    qb_, kt = halves[layer][c]
                    last = 8 if layer == 0 else 4 * qb_ + 4
                    n2 = cn2(layer, hB, c)
                    k = 2 * ch(layer, hB) + qb_
                    if kt == 0:
                        pe.wait_ge(o_copied, O_COPIED_0 + k)
                    if layer == 0:
                        q0 = 32 * (kt % 2)
                        mm(bank(OB)[64 + q0:96 + q0, :], vu[:, p, kt, :], nb[:, c % 2, :], start=kt < 2, stop=kt >= last - 2)
                    else:
                        q0 = 32 * (kt % 4)
                    pe.wait_ge(exp_ready, EXP_READY_0 + n2 + 1)
                    wide = 2 if layer == 0 else 4
                    ins = mm(bank(OB)[q0:q0 + 32, :], vg[:, p, kt, :], G[:, c % 2, :], start=kt < wide, stop=kt >= last - wide)
                    ins.then_inc(pv_done, 1)

                def final(hB, qb_):
                    k = 2 * ch(layer, hB) + qb_
                    pe.wait_ge(o_copied, O_COPIED_0 + k + 1)
                    if qb_ == 0:
                        pe.wait_ge(fin_done, FIN_DONE_0 + ch(layer, hB))
                    w = 18 if layer == 0 else 9
                    cc = C_SEL0 if layer == 0 else C_SEL1
                    for t in range(4):
                        q = qb_ * 4 + t
                        ins = mm(bank(XB)[:, q * 18:q * 18 + w], osb[:, t * P:(t + 1) * P], cst[:, cc:cc + w],
                                 start=True, stop=True)
                    ins.then_inc(fin_psum, 1)

                def half_step(hB, p, c, slot):
                    qb_, kt = halves[layer][c]
                    n2 = cn2(layer, hB, c)
                    kk, qq = kt * P, qb_ * 512
                    if layer == 0:
                        pe.wait_ge(n_ready, N_READY_0 + n2)
                        mm(bank(ZB), KT[0:ZROWS, slot, kk:kk + P], QT[0:ZROWS, slot, qq:qq + 512],
                           start=True, stop=True).then_inc(z_ready, 1)
                        pe.wait_ge(exp_ready, EXP_READY_0 + n2)
                        mm(bank(LB), KT[0:YROWS, slot, kk:kk + P], QT[0:YROWS, slot, qq:qq + 512], start=True, stop=False)
                        pe.wait_ge(n_ready, N_READY_0 + n2 + 1)
                        mm(bank(LB), negbig[:], nb[:, c % 2, :], start=False, stop=True).then_inc(l_ready, 1)
                    else:
                        pe.wait_ge(exp_ready, EXP_READY_0 + n2)
                        diag = kt >= 4 * qb_
                        ins = mm(bank(LB), KT[0:ZROWS, slot, kk:kk + P], QT[0:ZROWS, slot, qq:qq + 512],
                                 start=True, stop=not diag)
                        if diag:
                            off = (kt - 4 * qb_) * P
                            ins = mm(bank(LB), negbig[:], maskb[:, 384 - off:896 - off], start=False, stop=True)
                        ins.then_inc(l_ready, 1)
                    if c > 0:
                        product(hB, p, c - 1)

                def push_down(hA, i):
                    pe.wait_ge(ind_ready, hA * QT_TILES + i + 1)
                    for b2 in range(2):
                        ins = mm(bank(2 * (i % 2) + b2), negbig[:], ind[:, i % 2, b2 * 512:(b2 + 1) * 512],
                                 start=False, stop=True, skip_group_check=True)
                    ins.then_inc(masked, 1)

                def step(hA, p, hB):
                    pB = 1 - p
                    if hA is not None:
                        slotA = ch(layer, hA) % 4
                        loaded(pe, layer, hA, p)
                    if hB is not None:
                        slotB = ch(layer, hB) % 4
                    for i in range(QT_TILES):
                        if hA is not None:
                            n = cn(layer, hA, i)
                            if layer == 0 and i:
                                push_down(hA, i - 1)
                            pe.wait_ge(s_free, S_FREE_0 + n - 1)
                            width = SEQ if layer == 0 else (i + 1) * P
                            for b2 in range(2):
                                w = min(512, width - 512 * b2)
                                if w > 0:
                                    ins = mm(bank(2 * (i % 2) + b2)[:, 0:w], QT[0:CROWS, slotA, i * P:(i + 1) * P],
                                             KT[0:CROWS, slotA, b2 * 512:b2 * 512 + w], start=True, stop=True)
                            if layer == 1:
                                ins = mm(bank(2 * (i % 2) + i // 4)[:, (i % 4) * P:(i % 4 + 1) * P], negbig[:], upb[:],
                                         start=False, stop=True, skip_group_check=True)
                            ins.then_inc(s_ready, 1)
                        for c in (sched[layer][i] if hB is not None else []):
                            if c == 0:
                                pe.wait_ge(staged, 4 * (hB + 1) if layer == 0 else 4 * HB + hB + 1)
                                pe.wait_ge(tm_loaded, TM_LOADED_0 + 128 * (ch(layer, hB) + 1))
                            half_step(hB, pB, c, slotB)
                            if c == (10 if layer == 0 else 6):
                                final(hB, 0)
                    if hB is not None:
                        product(hB, pB, nh - 1)
                    if hA is not None:
                        if layer == 0:
                            push_down(hA, QT_TILES - 1)
                        if hB is not None:
                            pe.wait_ge(exp_ready, EXP_READY_0 + cn2(layer, hB, nh))
                        if layer == 0:
                            pe.wait_ge(bad_ready, BAD_READY_0 + hA + 1)
                            mm(bank(LB)[0:1, 0:QT_TILES + 1], ones[:, 0:1], badt[:], start=True, stop=True).then_inc(bad_psum, 1)
                            pe.wait_ge(bad_int, hA + 1)
                            settled(pe)
                            bad = pe.value_load(badi[0:1, QT_TILES:], min_val=0, max_val=P * QT_TILES)
                            with pe.If(bad > 0):
                                with pe.Fori(0, QT_TILES) as t:
                                    pe.wait_ge(fb_read, FB_READ_0 + hA * QT_TILES + t)
                                    settled(pe)
                                    bad_tile = pe.value_load(badi[0:1, bass.ds(t, 1)], min_val=0, max_val=P)
                                    with pe.If(bad_tile > 0):
                                        for b2 in range(2):
                                            ins = mm(bank(b2), QT[0:CROWS, slotA, bass.ds(t * P, P)],
                                                     KT[0:CROWS, slotA, b2 * 512:(b2 + 1) * 512], start=True, stop=True)
                                        ins.then_inc(fb_s, 1)
                                    with pe.Else():
                                        pe.sem_inc(fb_s, 1)
                            with pe.Else():
                                pe.sem_inc(fb_s, QT_TILES)
                        pe.wait_ge(tm_ready, ch(layer, hA) + 1)
                        settled(pe)
                        nc.tensor.transpose(bank(LB)[0:48, 0:64].bitcast(bf), tmp[:].rearrange("p t w r -> p (t w r)"),
                                            identb[:]).then_inc(tm_psum, 1)
                        pe.wait_ge(tm_copied, ch(layer, hA) + 1)
                    if hB is not None:
                        final(hB, 1)

                over_heads(pe, layer, step)

            pe.wait_ge(prep_done, 1)
            for k in range(TOPK):
                for fc in range(FC):
                    mm(bank(k)[:, fc * P:(fc + 1) * P], wi_sb[:, fc * P:(fc + 1) * P], ident, start=True, stop=False)
                    ins = mm(bank(k)[:, fc * P:(fc + 1) * P], la[:], lbs[:, k, fc * P:(fc + 1) * P], start=False, stop=True)
            ins.then_inc(ffw_psum, 1)
            mm(bank(2)[:, 0:1], ones[:], wabs[:], start=True, stop=True).then_inc(tern_psum, 1)
            pe.wait_ge(ffw_done, 2)
            for s in range(len(STAGES)):
                stage(s)
                if attention_of(s) is not None:
                    attention(attention_of(s))

        @block.vector
        def _(dve):
            V = nc.vector
            seq = Seq(dve, dve_seq)
            link = seq.link

            dve.wait_ge(const_in, 16 * 22)
            link(V.tensor_copy(identb[:], ident))
            link(V.tensor_scalar(negbig[:], ident, -BIG, None, ALU.mult))
            link(V.tensor_copy(upb[:], cst[:, C_UP:C_UP + P]))
            link(V.tensor_copy(maskb[:], cst[:, C_MASK:C_MASK + 896]))
            link(V.memset(ones[:], 1.0))
            link(V.memset(eps[:], EPS))
            link(V.memset(KT[:], 1.0))
            link(V.memset(QT[:], 0.0))
            link(V.memset(vg[:], 0.0))
            link(V.memset(vg[:, :, :, HD:HD + 1], 1.0))
            link(V.memset(vu[:], 0.0))
            link(V.memset(vu[:, :, :, 3 * HD:3 * HD + 1], 1.0))
            link(V.memset(tm[:], 0.0))
            link(V.tensor_copy(idxf[:], idx_sb[:]))
            for k in range(TOPK):
                link(V.tensor_scalar(esel[:, k:k + 1], idxf[:, k:k + 1], cst[:, C_EXP:C_EXP + 1], None, ALU.is_equal))
                link(V.tensor_scalar(lbs[:, k, :], lb[:], esel[:, k:k + 1], None, ALU.mult))
            link(V.tensor_reduce(wabs[:], wt_sb[:], AX.X, ALU.add, apply_absolute_value=True))
            link(V.memset(mark[:], 0.0))
            V.memset(mark[:], 0.0).then_inc(prep_done, 1)
            dve.wait_ge(ffw_psum, 1)
            V.tensor_copy(wk_ff[:], ps[:, 0:2, :]).then_inc(ffw_done, 1)
            dve.wait_ge(tern_psum, 1)
            link(V.tensor_scalar(wscale[:, 0:1], bank(2)[:, 0:1], 1.0 / (P * P), EPS, ALU.mult, ALU.max))
            link(V.tensor_scalar(wscale[:, 1:2], wscale[:, 0:1], 0.5, None, ALU.mult))
            link(V.tensor_scalar(wscale[:, 2:3], wscale[:, 0:1], -0.5, None, ALU.mult))
            link(V.tensor_scalar(wneg[:], wt_sb[:], wscale[:, 2:3], None, ALU.is_lt))
            link(V.scalar_tensor_tensor(wtern[:], wt_sb[:], wscale[:, 1:2], wneg[:], ALU.is_gt, ALU.subtract))
            V.tensor_scalar(wtern[:], wtern[:], wscale[:, 0:1], None, ALU.mult).then_inc(ffw_done, 1)
            dve.wait_ge(x_in_done, 16)

            LINKS = {("ffn", 0): 0, ("ffn", 1): 0, ("proj", 0): 0, ("proj", 1): 0, ("tern", 0): 0, ("tern", 1): 0,
                     ("qkv", 0): 35, ("qkv", 1): 26}

            def layer_norm(s):
                n = LN_OF[s]
                if X_BEFORE[s]:
                    dve.wait_ge(x_ready, X_READY_0 + 4 * X_BEFORE[s])
                with seq.loop(4, 4) as g:
                    for t in range(4):
                        link(V.bn_stats(stat[:, bass.ds(g * 4 + t, 1), :], x[:, bass.ds(g * 4 + t, 1), :]))
                me, m2e, mo, m2o = (stat[:, :, j] for j in (1, 2, 4, 5))
                link(V.tensor_tensor(ln[:, 0, :], me, mo, ALU.add))
                link(V.tensor_tensor(ln[:, 3, :], me, mo, ALU.subtract))
                link(V.tensor_tensor(ln[:, 1, :], m2e, m2o, ALU.add))
                link(V.tensor_tensor(ln[:, 3, :], ln[:, 3, :], ln[:, 3, :], ALU.mult))
                link(V.tensor_scalar(ln[:, 1, :], ln[:, 1, :], 1.0 / HID, None, ALU.mult))
                V.scalar_tensor_tensor(ln[:, 1, :], ln[:, 3, :], 0.25, ln[:, 1, :], ALU.mult, ALU.add).then_inc(var_ready, 1)
                dve.wait_ge(sd_ready, n + 1)
                link(V.reciprocal(ln[:, 4, :], ln[:, 2, :]))
                link(V.scalar_tensor_tensor(ln[:, 5, :], ln[:, 0, :], -0.5, ln[:, 4, :], ALU.mult, ALU.mult))

            def stage(s):
                kind, c, xo = STAGES[s]

                def make_h(g, half):
                    gg = 4 * s + g
                    dve.wait_ge(hT_ready, HT_READY_0 + gg - 1)
                    for t in range(4):
                        tile = bass.ds(g * 4 + t, 1)
                        o = h[:, half, t, :].rearrange("p (a d) -> p a d", a=1)
                        if kind == "proj":
                            ins = V.tensor_copy(o, ao[:, tile, :])
                        else:
                            ins = V.tensor_scalar(o, x[:, tile, :], ln[:, 4, tile], ln[:, 5, tile], ALU.mult, ALU.add)
                    ins.then_inc(h_ready, 1)

                def split(w):
                    a = qk_t[:, w, :]
                    r = res1[:, w, :]
                    link(V.tensor_copy(parts[:, w, 0, :], a))
                    link(V.tensor_tensor(r, a, parts[:, w, 0, :], ALU.subtract))
                    link(V.tensor_copy(parts[:, w, 1, :], r))
                    link(V.tensor_tensor(r, r, parts[:, w, 1, :], ALU.subtract))
                    V.tensor_copy(parts[:, w, 2, :], r).then_inc(part_ready, 1)

                def body(b, half):
                    g = b * 2 + half
                    make_h(g, half)
                    if xo is not None:
                        yy = 4 * xo + g
                    if kind == "ffn":
                        for fc in range(FC):
                            u = (c * 4 + g) * FC + fc
                            dve.wait_ge(a_psum, 2 * u + 2)
                            V.tensor_scalar(relu1[:, fc % 2, :], bank(2 + fc % 2), 0.0, val_sb[:, 1:2], ALU.max,
                                            ALU.mult).then_inc(relu1_ready, 1)
                            dve.wait_ge(relu1_ready, RELU1_READY_0 + u + 1)
                            dve.wait_ge(relu0_ready, RELU0_READY_0 + u + 1)
                            dve.wait_ge(y_psum, Y_PSUM_0 + yy)
                            V.scalar_tensor_tensor(mix[:, fc, :], relu0[:, fc % 2, :], val_sb[:, 0:1], relu1[:, fc % 2, :],
                                                   ALU.mult, ALU.add).then_inc(mix_ready, 1)
                    if xo is not None:
                        dve.wait_ge(y_psum, Y_PSUM_0 + yy + 1)
                        xt = x[:, bass.ds(g * 4, 4), :]
                        V.scalar_tensor_tensor(xt, bank(4 + half).rearrange("p (a d) -> p a d", a=4),
                                               1.0 if kind == "proj" else 0.5, xt, ALU.mult, ALU.add).then_inc(x_ready, 1)
                    if kind == "qkv":
                        kg = c * 4 + g
                        dve.wait_ge(part_stored, PART_STORED_0 + 32 * kg)
                        for w in range(2):
                            dve.wait_ge(qk_psum, 2 * kg + w + 1)
                            if c == 0:
                                V.tensor_scalar(qk_t[:, w, :], bank(w), bcol[:, w:w + 1], ISQ if w == 0 else 1.0,
                                                ALU.add, ALU.mult).then_inc(qk_read, 1)
                                dve.wait_ge(qk_read, QK_READ_0 + 2 * kg + w + 1)
                            else:
                                cos = cst[:, C_ROPE + half * 512:C_ROPE + half * 512 + 512]
                                sin = cst[:, C_ROPE + SEQ + half * 512:C_ROPE + SEQ + half * 512 + 512]
                                link(V.scalar_tensor_tensor(qk_t[:, w, :], bank(w), bcol[:, 2 + w:3 + w], cos, ALU.add, ALU.mult))
                                V.scalar_tensor_tensor(rot[:, w, :], bank(2 + w), bcol[:, 4 + w:5 + w], sin, ALU.add,
                                                       ALU.mult).then_inc(qk_read, 1)
                                dve.wait_ge(qk_read, QK_READ_0 + 2 * kg + w + 1)
                                link(V.tensor_tensor(qk_t[:, w, :], qk_t[:, w, :], rot[:, w, :], ALU.add))
                                if w == 0:
                                    link(V.tensor_scalar(qk_t[:, w, :], qk_t[:, w, :], ISQ, None, ALU.mult))
                            split(w)
                            if c == 0 and w == 0:
                                V.tensor_copy(qb[:, bass.ds(g * 4, 4), :],
                                              parts[:, 0, 0, :].rearrange("p (a d) -> p a d", a=4)).then_inc(qb_ready, 1)
                        if c == 0 and half == 1:
                            dve.wait_ge(kf_used, KF_USED_0 + g + 1)
                            link(V.tensor_copy(krow[0:1, 0, :], bank(2)[0:1, 0:P]))
                            link(V.tensor_copy(kcol[:], bank(3)[:, 0:1]))
                            V.tensor_scalar(krow[0:1, 1, :], krow[0:1, 0, :], -1.0 / SEQ, None, ALU.mult).then_inc(cov_row, 1)
                            dve.wait_ge(cov_full, b + 1)
                            link(V.tensor_tensor(cov[:, 0:P], bank(6)[:, 0:P], cst[:, C_HEAD:C_HEAD + P], ALU.mult))
                            V.tensor_scalar(cov[:, P:P + HEADS], cst[:, C_HSEL:C_HSEL + HEADS], kcol[:], None,
                                            ALU.mult).then_inc(cov_ready, 1)
                            for t in range(QT_TILES):
                                j = b * QT_TILES + t
                                bk = bank(2 + t % 2)
                                tile = bass.ds(j, 1)
                                dve.wait_ge(stat_psum, j + 1)
                                link(V.tensor_tensor(qc[:].rearrange("p (a d) -> p a d", a=1),
                                                     bk[:, 0:P].rearrange("p (a d) -> p a d", a=1), qtok[:, tile, :], ALU.mult))
                                V.tensor_copy(mu[:, tile, :], bk[:, P:P + HEADS].rearrange("p (a d) -> p a d", a=1)).then_inc(stat_read, 1)
                                link(V.tensor_reduce(sd[:, tile, :].rearrange("p a d -> p (a d)"), qc[:].rearrange("p (h d) -> p h d", d=HD), AX.X, ALU.add))

                groups(dve, seq, LINKS[kind, c], body)
                if kind == "qkv":
                    dve.wait_ge(tok_read, TOK_READ_0 + 16 * (c + 1))
                    if c == 0:
                        V.tensor_scalar(sd[:], sd[:], 1e-12, None, ALU.max).then_inc(sd2_var, 1)
                        dve.wait_ge(stat_read, STAT_READ_0 + TILES)
                        dve.wait_ge(sd2_ready, 1)
                        link(V.scalar_tensor_tensor(par[:, 0], sd[:], Z_START, mu[:], ALU.mult, ALU.add))
                        link(V.tensor_scalar(par[:, 1], sd[:], -0.5 / DENSITY1, None, ALU.mult))
                        link(V.tensor_scalar(par[:, 4], sd[:], -0.5 / DENSITY2, None, ALU.mult))
                        link(V.scalar_tensor_tensor(par[:, 2], sd[:], (SEQ / 2 - AIM1) / DENSITY1, par[:, 0], ALU.mult, ALU.add))
                        V.scalar_tensor_tensor(par[:, 3], sd[:], (SEQ / 2 - AIM2) / DENSITY2, par[:, 2], ALU.mult,
                                               ALU.add).then_inc(par_ready, 1)
                        link(V.tensor_copy(vp[:, 0], vf[:]))
                        link(V.tensor_tensor(vres[:], vf[:], vp[:, 0], ALU.subtract))
                        link(V.tensor_copy(vp[:, 1], vres[:]))
                        link(V.tensor_tensor(vres[:], vres[:], vp[:, 1], ALU.subtract))
                        link(V.tensor_copy(vp[:, 2], vres[:]))
                    V.memset(mark[:], 0.0).then_inc(v_ready, 1)

            def attention(layer):
                before = seq.k

                def below(hB, c):
                    n2 = cn2(0, hB, c)
                    dve.wait_ge(z_ready, n2 + 1)
                    dve.wait_ge(pv_done, PV_DONE_0 + n2 - 1)
                    V.tensor_scalar(nb[:, c % 2, :], bank(ZB), 0.0, None, ALU.is_lt).then_inc(n_ready, 1)

                def sort(hA, i):
                    dve.wait_ge(masked, hA * QT_TILES + i + 1)
                    settled(dve)
                    for sg in range(SEGS):
                        w = SEQ // SEGS
                        ins = V.max(cand[:, i, sg * 8:sg * 8 + 8], SA(i)[:, sg * w:(sg + 1) * w])
                    ins.then_inc(s_free, 1)
                    dve.wait_ge(s_free, S_FREE_0 + hA * QT_TILES + i + 1)
                    settled(dve)
                    link(V.max(srt[:, i, 1:9], cand[:, i, :]), plain=True)
                    link(V.match_replace(cand2[:, 0, :], srt[:, i, 1:9], cand[:, i, :], LOWEST), plain=True)
                    link(V.max(srt[:, i, 9:17], cand2[:, 0, :]), plain=True)
                    link(V.match_replace(cand2[:, 1, :], srt[:, i, 9:17], cand2[:, 0, :], LOWEST), plain=True)
                    link(V.max(srt[:, i, 17:25], cand2[:, 1, :]))

                def select(hA, p):
                    iota = cst[:, C_IOTA:C_IOTA + NSORT + 1]
                    shape = [P, QT_TILES, NSORT + 1]
                    it = iota.rearrange("p (a n) -> p a n", a=1).to_broadcast(shape)
                    at, hi, lo, lm, ok, thr = (sm[:, j, :] for j in range(6))
                    link(V.tensor_scalar(at, cnt[:], -1.0, float(KEEP), ALU.mult, ALU.add))
                    for o in (hi, lo):
                        link(V.tensor_tensor(sel[:], it, at.rearrange("p (t a) -> p t a", a=1).to_broadcast(shape), ALU.is_equal))
                        link(V.tensor_tensor(sel[:], sel[:], srt[:], ALU.mult))
                        link(V.tensor_reduce(o, sel[:], AX.X, ALU.add))
                        if o is hi:
                            link(V.tensor_scalar(at, at, 1.0, None, ALU.add))
                    link(V.tensor_reduce(lm, cand[:].rearrange("p t (s e) -> p t s e", e=8)[:, :, :, 7], AX.X, ALU.max))
                    link(V.tensor_tensor(ok, lo, lm, ALU.is_ge))
                    link(V.scalar_tensor_tensor(ok, at, 1.0, ok, ALU.is_ge, ALU.mult))
                    link(V.scalar_tensor_tensor(ok, at, float(NSORT), ok, ALU.is_le, ALU.mult))
                    link(V.tensor_scalar(badt[:, 0:QT_TILES], ok, -1.0, 1.0, ALU.mult, ALU.add))
                    V.tensor_reduce(badt[:, QT_TILES:], badt[:, 0:QT_TILES], AX.X, ALU.add).then_inc(bad_ready, 1)
                    dve.wait_ge(bad_psum, hA + 1)
                    V.tensor_copy(badi[:], bank(LB)[0:1, 0:QT_TILES + 1]).then_inc(bad_int, 1)
                    dve.wait_ge(bad_int, hA + 1)
                    settled(dve)
                    bad = dve.value_load(badi[0:1, QT_TILES:], min_val=0, max_val=P * QT_TILES)
                    rounds = KEEP // 8
                    per = 2 + 2 * rounds + 2
                    with dve.If(bad > 0):
                        with seq.loop(QT_TILES, per) as t:
                            bad_tile = dve.value_load(badi[0:1, bass.ds(t, 1)], min_val=0, max_val=P)
                            with dve.If(bad_tile > 0):
                                dve.wait_ge(fb_s, hA * QT_TILES + t + 1)
                                V.tensor_copy(fw[:], SA(0)).then_inc(fb_read, 1)
                                dve.wait_ge(fb_read, FB_READ_0 + hA * QT_TILES + t + 1)
                                link(V.memset(fm[:], 0.0), plain=True)
                                with seq.loop(rounds, 2):
                                    link(V.max(fm[:], fw[:]), plain=True)
                                    link(V.match_replace(fw[:], fm[:], fw[:], LOWEST), plain=True)
                                link(V.max(fm[:], fw[:]))
                                r = KEEP - 8 * rounds
                                link(V.tensor_copy(sm[:, 1, bass.ds(t, 1)], fm[:, r - 1:r]))
                                link(V.tensor_copy(sm[:, 2, bass.ds(t, 1)], fm[:, r:r + 1]), plain=True)
                            with dve.Else():
                                dve.sem_inc(fb_read, 1)
                                dve.sem_inc(dve_seq, per)
                    with dve.Else():
                        dve.sem_inc(fb_read, QT_TILES)
                        dve.sem_inc(dve_seq, QT_TILES * per)
                    link(V.tensor_tensor(thr, hi, lo, ALU.add))
                    link(V.tensor_scalar(tm[:, :, 0], thr, -0.5, None, ALU.mult))
                    V.tensor_scalar(sm[:, 6 + p, :], rmax[:, p, :], 0.0, None, ALU.max).then_inc(mx_ready, 1)
                    dve.wait_ge(mx_ready, hA + 1)
                    link(V.scalar_tensor_tensor(tm[:, :, 1], thr, 0.5, sm[:, 6 + p, :], ALU.mult, ALU.subtract))

                def split_rows(hA):
                    link(V.tensor_copy(tmp[:, :, :, 0], tm[:]))
                    link(V.tensor_tensor(tmr[:, 0], tm[:], tmp[:, :, :, 0], ALU.subtract))
                    link(V.tensor_copy(tmp[:, :, :, 1], tmr[:, 0]))
                    link(V.tensor_tensor(tmr[:, 1], tmr[:, 0], tmp[:, :, :, 1], ALU.subtract))
                    ins = V.tensor_copy(tmp[:, :, :, 2], tmr[:, 1])
                    ins.then_inc(tm_ready, 1)

                def finish(hB, p):
                    n = ch(layer, hB)
                    dve.wait_ge(fin_psum, FIN_PSUM_0 + 2 * (n + 1))
                    fp = bank(XB)[:, 0:144].rearrange("p (t c) -> p t c", c=18)
                    if layer == 0:
                        dve.wait_ge(em_ready, hB + 1)
                        link(V.tensor_tensor(fin[:, 0], fp[:, :, 9:18],
                                             em[:, p, :].rearrange("p (t a) -> p t a", a=1).to_broadcast([P, QT_TILES, 9]), ALU.mult))
                        ins = V.tensor_tensor(fin[:, 1], fp[:, :, 0:9], fin[:, 0], ALU.add)
                    else:
                        ins = V.tensor_copy(fin[:, 1], fp[:, :, 0:9])
                    ins.then_inc(fin_done, 1)
                    dve.wait_ge(fin_done, FIN_DONE_0 + n + 1)
                    link(V.reciprocal(frec[:], fin[:, 1, :, 8]))
                    b, hd = hB // HEADS, hB % HEADS
                    link(V.tensor_tensor(ao[:, bass.ds(b * QT_TILES, QT_TILES), bass.ds(hd * HD, HD)], fin[:, 1, :, 0:HD],
                                         frec[:].rearrange("p (t a) -> p t a", a=1).to_broadcast([P, QT_TILES, HD]), ALU.mult))

                def step(hA, p, hB):
                    for i in range(QT_TILES):
                        cs_ = sched[layer][i] if hB is not None and layer == 0 else []
                        if hA is not None:
                            n = cn(layer, hA, i)
                            dve.wait_ge(s_ready, n + 1)
                            width = SEQ if layer == 0 else (i + 1) * P
                            ins = V.tensor_reduce(rmax[:, p, i:i + 1], SA(i)[:, 0:width], AX.X, ALU.max)
                            ins.then_inc(rmax_done if layer == 0 else s_free, 1)
                        for c in cs_[:1]:
                            below(hB, c)
                        if hA is not None and layer == 0 and i:
                            sort(hA, i - 1)
                        for c in cs_[1:]:
                            below(hB, c)
                        if hA is not None and layer == 0:
                            dve.wait_ge(t2_ready, hA * QT_TILES + i + 1)
                            V.tensor_scalar(ind[:, i % 2, :], SA(i), srt[:, i, 0:1], None, ALU.is_ge, ALU.add,
                                            accum_out=cnt[:, i:i + 1]).then_inc(ind_ready, 1)
                    if hA is not None and layer == 0:
                        sort(hA, QT_TILES - 1)
                        select(hA, p)
                        split_rows(hA)
                    if hA is not None and layer == 1:
                        dve.wait_ge(s_free, S_FREE_0 + cn(1, hA, QT_TILES))
                        link(V.tensor_scalar(tm[:, :, 0], rmax[:, p, :], -1.0, None, ALU.mult))
                        split_rows(hA)
                    if hB is not None:
                        finish(hB, 1 - p)

                step(0, 0, None)
                per = 2 * (seq.k - before + (3 if layer == 0 else 2))
                with seq.loop((HB - 2) // 2, per) as i:
                    step(i * 2 + 1, 1, i * 2)
                    step(i * 2 + 2, 0, i * 2 + 1)
                step(HB - 1, 1, HB - 2)
                step(None, 0, HB - 1)

            for s in range(len(STAGES)):
                if s in LN_OF:
                    layer_norm(s)
                stage(s)
                if attention_of(s) is not None:
                    attention(attention_of(s))


def kernel(**inputs):
    import concourse.bacc as bacc
    from concourse.bass_utils import run_bass_kernel_spmd as run

    a = {k: np.asarray(v) for k, v in inputs.items()}
    swap = np.arange(HID) ^ 1
    l0, l1 = "L0_attn_", "L1_attn_"
    host = {
        "consts": shape_constants(),
        "x_in": a["L0_attn_x"].reshape(BATCH * SEQ, HID),
        "wq0": a[l0 + "Wq"], "wk0": a[l0 + "Wk"], "wv0": a[l0 + "Wv"], "wo0": a[l0 + "Wo"],
        "rows0": np.stack([a[l0 + "b" + c] for c in "qkvo"])[None],
        "cols0": np.stack([a[l0 + "b" + c] for c in "qk"], 1),
        "wi": a["L0_ffn_wi_w"].reshape(FC, P, HID).transpose(1, 0, 2).reshape(P, FF),
        "wo_ff": a["L0_ffn_wo_w"].T.reshape(FC, P, HID).transpose(1, 0, 2),
        "lora_a": a["L0_ffn_lora_As"].reshape(EXPERTS * RANK, HID),
        "lora_b": a["L0_ffn_lora_Bs"].transpose(0, 2, 1).reshape(EXPERTS * RANK, FF),
        "idx": np.broadcast_to(a["L0_ffn_top_k_indices"], (P, TOPK)),
        "val": np.broadcast_to(a["L0_ffn_top_k_values"], (P, TOPK)),
        "wq1": a[l1 + "Wq"], "wk1": a[l1 + "Wk"], "wv1": a[l1 + "Wv"], "wo1": a[l1 + "Wp"],
        "rows1": np.stack([a[l1 + "b" + c] for c in "qkvp"])[None],
        "cols1": np.stack([a[l1 + "bq"], a[l1 + "bk"], a[l1 + "bq"][swap], a[l1 + "bk"][swap]], 1),
        "wq1s": a[l1 + "Wq"][:, swap], "wk1s": a[l1 + "Wk"][:, swap],
        "wt": a["L1_ffn_weight"].T,
    }
    nc = bacc.Bacc("TRN2", target_bir_lowering=False, num_devices=1)
    arrays, args = {}, {}
    for name, v in host.items():
        v = np.ascontiguousarray(v)
        arrays["in_" + name] = v
        args[name] = nc.dram_tensor("in_" + name, v.shape, mybir.dt.from_np(v.dtype), kind="ExternalInput").ap()
    for name in ("qs", "ks"):
        args[name] = nc.dram_tensor(name, (BATCH, 3, HID, SEQ), mybir.dt.bfloat16, kind="Internal").ap()
    args["out"] = nc.dram_tensor("out_x", (BATCH * SEQ, HID), mybir.dt.float32, kind="ExternalOutput").ap()
    macaron_kernel(nc, **args)
    r = run(nc, [arrays], core_ids=[0])
    return r.results[0]["out_x"].reshape(BATCH, SEQ, HID)
```

```python
import numpy as np
from contextlib import ExitStack, contextmanager

import concourse.bass as bass
from concourse import mybir

P = 128
BATCH, SEQ, HID = 2, 1024, 128
HEADS, HD = 16, 8
TILES = BATCH * SEQ // P
QT_TILES = SEQ // P
HB = BATCH * HEADS
FF, EXPERTS, RANK, TOPK = 512, 8, 16, 2
FC = FF // P
KEEP = int(SEQ * (1.0 - 0.9))
EPS = 1e-5
BIG = 2.0 ** 100
LOWEST = -3.0e38
CROWS = 9 * HD
ZROWS, YROWS = CROWS + 3, CROWS + 6
Z_START = 1.29
AIM1, AIM2 = 93, 91
DENSITY1, DENSITY2 = 195.0, 230.0
NSORT = 24
SEGS = 8
ISQ = float(1.0 / np.sqrt(np.float32(HD)))

C_ID, C_UP, C_HEAD, C_MASK = 0, 128, 256, 384
C_HSEL = C_MASK + P
C_EXP = C_HSEL + HEADS
C_SEL0 = C_EXP + 1
C_SEL1 = C_SEL0 + 18
C_IOTA = C_SEL1 + 9
C_ROPE = C_IOTA + NSORT + 1
C_ALL = C_ROPE + 2 * SEQ


def shape_constants():
    c = np.zeros((P, C_ALL), np.float32)
    r = np.arange(P)
    c[:, C_ID:C_ID + P] = np.eye(P)
    c[:, C_UP:C_UP + P] = r[None, :] > r[:, None]
    c[:, C_HEAD:C_HEAD + P] = (r[:, None] // HD == r[None, :] // HD) / SEQ
    c[:, C_MASK:C_MASK + P] = r[:, None] > r[None, :]
    c[:, C_HSEL:C_HSEL + HEADS] = (r[:, None] // HD == np.arange(HEADS)[None, :]) / SEQ
    c[:, C_EXP] = r // RANK
    for d in range(HD + 1):
        for quad in (0, 1):
            c[32 * quad + d, C_SEL0 + d] = 1
        for quad in (2, 3):
            for part in range(3 if d < HD else 1):
                row = part * HD + d if d < HD else 3 * HD
                c[32 * quad + row, C_SEL0 + 9 + d] = 1 if quad == 2 else -0.5
        for quad in range(4):
            c[32 * quad + d, C_SEL1 + d] = 1
    c[:, C_IOTA:C_IOTA + NSORT + 1] = np.arange(NSORT + 1)
    half = HD // 2
    inv = (1.0 / np.float32(10000.0) ** (np.arange(half, dtype=np.float32) * np.float32(2.0) / np.float32(HD))).astype(np.float32)
    ang = np.arange(SEQ, dtype=np.float32)[:, None] * inv[None, :]
    freq = (r % HD) // 2
    c[:, C_ROPE:C_ROPE + SEQ] = np.cos(ang).T[freq]
    c[:, C_ROPE + SEQ:] = np.sin(ang).T[freq] * np.where(r % 2 == 0, -1.0, 1.0)[:, None]
    return c


def macaron_kernel(nc, consts, x_in, wq0, wk0, wv0, wo0, rows0, cols0, wi, wo_ff, lora_a, lora_b, idx, val,
                   wq1, wk1, wv1, wo1, rows1, cols1, wq1s, wk1s, wt, qs, ks, tms, out):
    f32, bf, i32 = mybir.dt.float32, mybir.dt.bfloat16, mybir.dt.int32
    ALU, ACT, AX = mybir.AluOpType, mybir.ActivationFunctionType, mybir.AxisListType
    ctx = ExitStack()
    with ctx:
        def sb(name, shape, dt=f32):
            return ctx.enter_context(nc.sbuf_tensor(name, shape, dt))

        def sem(name):
            return ctx.enter_context(nc.semaphore(name))

        x = sb("x", [P, TILES, HID])
        ao = sb("ao", [P, TILES, HID])
        cst = sb("cst", [P, C_ALL])
        ident = cst[:, C_ID:C_ID + P]
        identb = sb("identb", [P, P], bf)
        negbig = sb("negbig", [P, P], bf)
        halfbig = sb("halfbig", [P, P], bf)
        minus = sb("minus", [1, P], bf)
        onesb = sb("onesb", [1, 512], bf)
        tiny = sb("tiny", [P, 1])
        vhalf = sb("vhalf", [P, HB, HD + 1])
        upb = sb("upb", [P, P], bf)
        maskb = sb("maskb", [P, P], bf)
        ones = sb("ones", [P, P])
        w0 = sb("w0", [P, 3, P]); w1 = sb("w1", [P, 3, P])
        w1s = sb("w1s", [P, 2, P])
        wo_a = sb("wo_a", [P, 2, P])
        brow = sb("brow", [1, 2, 4, P])
        bcol = sb("bcol", [P, 8])
        la = sb("la", [P, P]); lb = sb("lb", [P, FF]); lbs = sb("lbs", [P, TOPK, FF])
        wi_sb = sb("wi_sb", [P, FF]); wo_sb = sb("wo_sb", [P, FC, P])
        idx_sb = sb("idx_sb", [P, TOPK], i32); idxf = sb("idxf", [P, TOPK]); esel = sb("esel", [P, TOPK])
        val_sb = sb("val_sb", [P, TOPK])
        wk_ff = sb("wk_ff", [P, TOPK, FF])
        wt_sb = sb("wt_sb", [P, P]); wtern = sb("wtern", [P, P]); wneg = sb("wneg", [P, P])
        wabs = sb("wabs", [P, 1]); wscale = sb("wscale", [P, 3])
        stat = sb("stat", [P, TILES, 6]); ln = sb("ln", [P, 6, TILES])
        eps = sb("eps", [P, 1])
        h = sb("h", [P, 2, 4, P]); hT = sb("hT", [P, 2, 4 * P])
        relu0 = sb("relu0", [P, 2, 4 * P]); relu1 = sb("relu1", [P, 2, 4 * P]); mix = sb("mix", [P, FC, 4 * P])
        qk_t = sb("qk_t", [P, 2, 4 * P]); res1 = sb("res1", [P, 2, 4 * P])
        rot = sb("rot", [P, 2, 4 * P])
        parts = sb("parts", [P, 2, 3, 4 * P], bf)
        qb = sb("qb", [P, TILES, HID], bf)
        qtok = sb("qtok", [P, TILES, HID], bf)
        kf = sb("kf", [P, 4, P])
        vf = sb("vf", [P, TILES, HID]); vres = sb("vres", [P, TILES, HID])
        vp = sb("vp", [P, 3, TILES, HID], bf)
        krow = sb("krow", [1, 2, P]); kcol = sb("kcol", [P, 1]); cov = sb("cov", [P, 144], bf)
        qc = sb("qc", [P, HID])
        mu = sb("mu", [P, TILES, HEADS]); sd = sb("sd", [P, TILES, HEADS]); par = sb("par", [P, 5, TILES, HEADS])
        QT = sb("QT", [P, 4, SEQ], bf); KT = sb("KT", [P, 4, SEQ], bf)
        pst = sb("pst", [P, 2, 5, QT_TILES])
        vg = sb("vg", [P, 2, QT_TILES, 32]); vu = sb("vu", [P, 2, QT_TILES, 32], bf)
        rmax = sb("rmax", [P, 2, QT_TILES]); cs = sb("cs", [P, 2, 2])
        t1 = sb("t1", [P, 2]); off2 = sb("off2", [P, 2]); cnt = sb("cnt", [P, 2, QT_TILES])
        junk = sb("junk", [P, 2, SEQ], bf); ind = sb("ind", [P, 2, SEQ], bf)
        cand = sb("cand", [P, 2, QT_TILES, SEGS * 8]); cand2 = sb("cand2", [P, 2, SEGS * 8])
        srt = sb("srt", [P, 2, QT_TILES, NSORT + 1])
        sel = sb("sel", [P, QT_TILES, NSORT + 1]); sm = sb("sm", [P, 12, QT_TILES])
        tm = sb("tm", [P, QT_TILES, 2]); tmr = sb("tmr", [P, 2, QT_TILES, 2])
        tmp = sb("tmp", [P, QT_TILES, 2, 3], bf); tmT = sb("tmT", [48, P], bf)
        em = sb("em", [P, 2, QT_TILES]); badt = sb("badt", [P, QT_TILES + 1]); badi = sb("badi", [1, QT_TILES + 1], i32)
        sgn = sb("sgn", [P, 4, 512], bf); G = sb("G", [P, 4, 512]); osb = sb("osb", [P, 512])
        fin = sb("fin", [P, 2, QT_TILES, 9]); frec = sb("frec", [P, QT_TILES])
        mark = sb("mark", [1, 2])
        fw = sb("fw", [P, SEQ]); fm = sb("fm", [P, 8])
        ps = ctx.enter_context(nc.psum_tensor("ps", [P, 8, 512], f32))

        const_in = sem("const_in")
        x_in_done = sem("x_in_done")
        out_done = sem("out_done")
        passed = sem("passed")
        dve_seq = sem("dve_seq")
        pool_seq = sem("pool_seq")
        prep_done = sem("prep_done")
        ffw_psum = sem("ffw_psum")
        ffw_done = sem("ffw_done")
        tern_psum = sem("tern_psum")
        var_ready = sem("var_ready")
        sd_ready = sem("sd_ready")
        h_ready = sem("h_ready")
        hT_psum = sem("hT_psum")
        hT_ready = sem("hT_ready")
        a_psum = sem("a_psum")
        relu0_ready = sem("relu0_ready")
        relu1_ready = sem("relu1_ready")
        mix_ready = sem("mix_ready")
        y_psum = sem("y_psum")
        x_ready = sem("x_ready")
        qk_psum = sem("qk_psum")
        qk_read = sem("qk_read")
        part_ready = sem("part_ready")
        part_stored = sem("part_stored")
        tok_psum = sem("tok_psum")
        tok_read = sem("tok_read")
        kf_ready = sem("kf_ready")
        kf_used = sem("kf_used")
        cov_row = sem("cov_row")
        cov_full = sem("cov_full")
        cov_ready = sem("cov_ready")
        qb_ready = sem("qb_ready")
        stat_psum = sem("stat_psum")
        stat_read = sem("stat_read")
        sd2_var = sem("sd2_var")
        sd2_ready = sem("sd2_ready")
        par_ready = sem("par_ready")
        qk_loaded0 = sem("qk_loaded0")
        qk_loaded1 = sem("qk_loaded1")
        staged = sem("staged")
        s_ready = sem("s_ready")
        c0_done = sem("c0_done")
        t1_ready = sem("t1_ready")
        c1_done = sem("c1_done")
        t2_ready = sem("t2_ready")
        ind_ready = sem("ind_ready")
        masked = sem("masked")
        bad_ready = sem("bad_ready")
        bad_psum = sem("bad_psum")
        bad_int = sem("bad_int")
        fb_s = sem("fb_s")
        fb_read = sem("fb_read")
        tm_ready = sem("tm_ready")
        tm_psum = sem("tm_psum")
        tm_copied = sem("tm_copied")
        tm_stored = sem("tm_stored")
        tm_loaded = sem("tm_loaded")
        mx_ready = sem("mx_ready")
        em_ready = sem("em_ready")
        pst_ready = sem("pst_ready")
        v_ready = sem("v_ready")
        s_free = sem("s_free")
        vsum_psum = sem("vsum_psum")
        z_ready = sem("z_ready")
        n_ready = sem("n_ready")
        l_ready = sem("l_ready")
        exp_ready = sem("exp_ready")
        pv_done = sem("pv_done")
        o_copied = sem("o_copied")
        fin_psum = sem("fin_psum")
        fin_done = sem("fin_done")

        HT_READY_0 = 2
        RELU0_READY_0 = 2
        RELU1_READY_0 = 2
        MIX_READY_0 = 2
        Y_PSUM_0 = 1
        X_READY_0 = 2
        QK_READ_0 = 2
        PART_STORED_0 = 32
        TOK_READ_0 = 2
        KF_USED_0 = 1
        STAT_READ_0 = 2
        L_READY_0 = 33
        S_FREE_0 = 2
        N_READY_0 = 1
        EXP_READY_0 = 1
        PV_DONE_0 = 18
        FB_READ_0 = 1
        O_COPIED_0 = 1
        FIN_PSUM_0 = 1
        FIN_DONE_0 = 1
        TM_STORED_0 = 16
        TM_LOADED_0 = 16
        BAD_READY_0 = 2

        def settled(eng):
            eng.sem_inc(passed, 1)

        class Seq:
            def __init__(self, eng, counter):
                self.eng, self.s, self.n, self.k = eng, counter, 0, 0

            def count(self, ins):
                self.n, self.k = self.n + 1, self.k + 1
                ins.then_inc(self.s, 1)

            def link(self, ins, plain=False):
                self.count(ins)
                self.eng.wait_ge(self.s, self.n)
                if plain:
                    settled(self.eng)

            @contextmanager
            def loop(self, count, per):
                start, k = self.n, self.k
                with self.eng.Fori(0, count) as i:
                    self.n = start + i * per
                    yield i
                assert self.k - k == per, (self.k - k, per)
                self.n, self.k = start + count * per, k + per * count

        HALVES0 = [(q, k) for q in range(2) for k in range(8)]
        HALVES1 = [(q, k) for q in range(2) for k in range(4 * q + 4)]
        PERIODS0 = [[2 * i, 2 * i + 1] for i in range(QT_TILES)]
        PERIODS1 = [[0, 1], [2], [3, 4], [5], [6, 7], [8], [9, 10], [11]]
        halves = {0: HALVES0, 1: HALVES1}
        periods = {0: PERIODS0, 1: PERIODS1}
        WIDE = {0: 2, 1: 4}
        TURN = {0: 8, 1: 4}
        base_n = [0, HB * QT_TILES]
        base_n2 = [0, HB * 16]

        def first_query(layer, c):
            qb, kt = halves[layer][c]
            return max(kt - 4 * qb, 0) * P if layer else 0

        def cn(layer, hb, i):
            return base_n[layer] + hb * QT_TILES + i

        def cn2(layer, hb, c):
            return base_n2[layer] + hb * len(halves[layer]) + c

        def ch(layer, hb):
            return layer * HB + hb

        def over_steps(step, loop):
            step(0, 0, "AN")
            step(1, 1, "ANSM")
            step(2, 0, "ANSMB")
            with loop() as i:
                step(i * 2 + 3, 1, "ANSMBP")
                step(i * 2 + 4, 0, "ANSMBP")
            step(HB - 1, 1, "ASMBP")
            step(HB, 0, "SMBP")
            step(HB + 1, 1, "BP")
            step(HB + 2, 0, "P")

        LOOPS = (HB - 4) // 2

        def loaded(eng, layer, hb, p):
            eng.wait_ge((qk_loaded0, qk_loaded1)[p], 96 * (layer * HB // 2 + (hb - p) // 2 + 1))

        def bank(i):
            return ps[:, i, :]

        def SA(i):
            return ps[:, 2 * (i % 2):2 * (i % 2) + 2, :].rearrange("p a b -> p (a b)")

        ZB, LB, OB, XB = 4, 5, 6, 7
        TM_PERIOD = {0: 5, 1: 3}

        def lbank(layer, c):
            return bank(LB if layer == 0 else ZB + c % 2)

        block = ctx.enter_context(nc.Block())

        @block.sync
        def _(sp):
            sp.dma_start(x[:], x_in.rearrange("(t p) d -> p t d", p=P)).then_inc(x_in_done, 16)
            for dst, src in ((cst[:], consts), (la[:], lora_a), (lb[:], lora_b), (wi_sb[:], wi),
                             (wo_sb[:], wo_ff), (idx_sb[:], idx), (val_sb[:], val), (wt_sb[:], wt),
                             (w0[:, 0, :], wq0), (w0[:, 1, :], wk0), (w0[:, 2, :], wv0), (wo_a[:, 0, :], wo0),
                             (w1[:, 0, :], wq1), (w1[:, 1, :], wk1), (w1[:, 2, :], wv1), (wo_a[:, 1, :], wo1),
                             (w1s[:, 0, :], wq1s), (w1s[:, 1, :], wk1s),
                             (brow[0:1, 0, :, :], rows0), (brow[0:1, 1, :, :], rows1),
                             (bcol[:, 0:2], cols0), (bcol[:, 2:6], cols1)):
                sp.dma_start(dst, src).then_inc(const_in, 16)

            sp.wait_ge(prep_done, 1)
            for layer in range(2):
                with sp.Fori(0, 2) as b:
                    for half in range(2):
                        kg = layer * 4 + b * 2 + half
                        sp.wait_ge(part_ready, 2 * (kg + 1))
                        for w, scr in ((0, qs), (1, ks)):
                            sp.dma_start(scr[b, :, :, half * 512:(half + 1) * 512].rearrange("a f t -> f a t"),
                                         parts[:, w, :, :]).then_inc(part_stored, 16)
                sp.wait_ge(part_stored, PART_STORED_0 + 32 * (layer * 4 + 4))

                def load(hb, p):
                    slot = ch(layer, hb) % 4
                    rows = bass.ds((hb % HEADS) * HD, HD)
                    for i in range(3):
                        block3 = slice(3 * HD * i, 3 * HD * (i + 1))
                        sp.dma_start(QT[block3, slot, :],
                                     qs[hb // HEADS, i, rows, :].rearrange("(a f) t -> a f t", a=1)
                                     .to_broadcast([3, HD, SEQ])).then_inc((qk_loaded0, qk_loaded1)[p], 16)
                        sp.dma_start(KT[block3, slot, :], ks[hb // HEADS, :, rows, :]
                                     ).then_inc((qk_loaded0, qk_loaded1)[p], 16)

                load(0, 0)

                def step(s, p, has):
                    if "N" in has:
                        sp.wait_ge(l_ready, L_READY_0 + cn2(layer, s - 2, 0))
                        if not (isinstance(s, int) and s == 0):
                            loaded(sp, layer, s - 1, 1 - p)
                        load(s + 1, 1 - p)
                    if "S" in has:
                        k = ch(layer, s - 1)
                        sp.wait_ge(tm_copied, k + 1)
                        sp.wait_ge(tm_loaded, TM_LOADED_0 + 16 * k)
                        sp.dma_start(tms.rearrange("r (t c) -> t r c", c=P), tmT[:]).then_inc(tm_stored, 16)
                        sp.wait_ge(tm_stored, TM_STORED_0 + 16 * (k + 1))
                        sp.dma_start(QT[CROWS:YROWS, k % 4, :], tms).then_inc(tm_loaded, 16)

                over_steps(step, lambda: sp.Fori(0, LOOPS))

            sp.wait_ge(x_ready, X_READY_0 + 4 * 6)
            sp.dma_start(out.rearrange("(t p) d -> p t d", p=P), x[:]).then_inc(out_done, 16)
            sp.wait_ge(out_done, 16)

        STAGES = [("ffn", 0, 0), ("qkv", 0, None), ("proj", 0, 1), ("ffn", 1, 2),
                  ("tern", 0, 3), ("qkv", 1, None), ("proj", 1, 4), ("tern", 1, 5)]
        LN_OF = {0: 0, 1: 1, 3: 2, 4: 3, 5: 4, 7: 5}
        X_BEFORE = {0: 0, 1: 1, 3: 2, 4: 3, 5: 4, 7: 5}

        def groups(eng, seq, per, prepare, body):
            with (eng.Fori(0, 2) if seq is None else seq.loop(2, per)) as b:
                for part in (prepare, body):
                    for half in range(2):
                        part(b, half)

        def attention_of(s):
            return {1: 0, 5: 1}.get(s)

        @block.gpsimd
        def _(pool):
            for counter, start in (
                    (hT_ready, HT_READY_0), (relu0_ready, RELU0_READY_0), (relu1_ready, RELU1_READY_0), (mix_ready, MIX_READY_0),
                    (y_psum, Y_PSUM_0), (x_ready, X_READY_0), (qk_read, QK_READ_0), (part_stored, PART_STORED_0),
                    (tok_read, TOK_READ_0), (kf_used, KF_USED_0), (stat_read, STAT_READ_0), (l_ready, L_READY_0),
                    (s_free, S_FREE_0), (n_ready, N_READY_0), (exp_ready, EXP_READY_0), (pv_done, PV_DONE_0),
                    (fb_read, FB_READ_0), (o_copied, O_COPIED_0), (fin_psum, FIN_PSUM_0), (fin_done, FIN_DONE_0),
                    (tm_stored, TM_STORED_0), (tm_loaded, TM_LOADED_0), (bad_ready, BAD_READY_0),
            ):
                pool.sem_inc(counter, start)
            pool.wait_ge(prep_done, 1)
            for layer in range(2):
                if layer == 0:
                    pool.wait_ge(par_ready, 1)
                pool.wait_ge(v_ready, layer + 1)

                def parameters(h, p):
                    for k in range(5):
                        ins = nc.gpsimd.tensor_copy(pst[:, p, k, :].rearrange("p (t a) -> p t a", a=1),
                                                    par[:, k, bass.ds((h // HEADS) * QT_TILES, QT_TILES), bass.ds(h % HEADS, 1)])
                    ins.then_inc(pst_ready, 1)

                def values(h, p):
                    tl, fd = bass.ds((h // HEADS) * QT_TILES, QT_TILES), bass.ds((h % HEADS) * HD, HD)
                    pool.wait_ge(pv_done, PV_DONE_0 + cn2(layer, h - 1, 0))
                    nc.gpsimd.tensor_copy(vg[:, p, :, 0:HD], vf[:, tl, fd]).then_inc(staged, 1)
                    if layer == 0:
                        for part in range(3):
                            nc.gpsimd.tensor_copy(vu[:, p, :, part * HD:(part + 1) * HD],
                                                  vp[:, part, tl, fd]).then_inc(staged, 1)

                def thresholds(h, p, i):
                    n = h * QT_TILES + i
                    c0, c1 = cs[:, 0, i % 2:i % 2 + 1], cs[:, 1, i % 2:i % 2 + 1]
                    pool.wait_ge(c0_done, n + 1)
                    settled(pool)
                    nc.gpsimd.tensor_scalar(t1[:, i % 2:i % 2 + 1], c0, pst[:, p, 1, i:i + 1],
                                            pst[:, p, 2, i:i + 1], ALU.mult, ALU.add).then_inc(t1_ready, 1)
                    nc.gpsimd.tensor_scalar(off2[:, i % 2:i % 2 + 1], c0, pst[:, p, 1, i:i + 1],
                                            pst[:, p, 3, i:i + 1], ALU.mult, ALU.add).then_inc(pool_seq, 1)
                    pool.wait_ge(pool_seq, n + 1)
                    pool.wait_ge(bad_ready, BAD_READY_0 + h - 1)
                    pool.wait_ge(c1_done, n + 1)
                    settled(pool)
                    nc.gpsimd.tensor_scalar(srt[:, p, i, 0:1], c1, pst[:, p, 4, i:i + 1],
                                            off2[:, i % 2:i % 2 + 1], ALU.mult, ALU.add).then_inc(t2_ready, 1)

                def step(s, p, has):
                    if layer == 0 and "N" in has:
                        parameters(s + 1, 1 - p)
                    if "S" in has:
                        values(s - 1, 1 - p)
                    if layer == 0:
                        for i in range(QT_TILES):
                            if "A" in has and i < QT_TILES - 1:
                                thresholds(s, p, i + 1)
                            if "N" in has and i == QT_TILES - 1:
                                thresholds(s + 1, 1 - p, 0)

                if layer == 0:
                    parameters(0, 0)
                    thresholds(0, 0, 0)
                over_steps(step, lambda: pool.Fori(0, LOOPS))

        @block.scalar
        def _(act):
            def layer_norm(s):
                n = LN_OF[s]
                act.wait_ge(var_ready, n + 1)
                nc.scalar.activation(ln[:, 2, :], ln[:, 1, :], ACT.Sqrt, bias=eps[:]).then_inc(sd_ready, 1)

            def stage(s):
                kind, c, xo = STAGES[s]

                def prepare(b, half):
                    act.wait_ge(hT_psum, 4 * s + b * 2 + half + 1)
                    nc.scalar.activation(hT[:, half, :], bank(XB), ACT.Copy).then_inc(hT_ready, 1)

                def body(b, half):
                    g = b * 2 + half
                    if kind == "ffn":
                        for fc in range(FC):
                            u = (c * 4 + g) * FC + fc
                            act.wait_ge(a_psum, 2 * u + 1)
                            act.wait_ge(mix_ready, MIX_READY_0 + u - 1)
                            nc.scalar.activation(relu0[:, fc % 2, :], bank(fc % 2), ACT.Relu).then_inc(relu0_ready, 1)
                    if kind == "qkv":
                        kg = c * 4 + g
                        for t in range(4):
                            act.wait_ge(tok_psum, kg * 4 + t + 1)
                            tile = bass.ds(g * 4 + t, 1)
                            bk = bank(4 + t % 2)
                            if c == 0:
                                nc.scalar.activation(qtok[:, tile, :], bk[:, 0:P].rearrange("p (a d) -> p a d", a=1),
                                                     ACT.Copy, scale=ISQ)
                                if t == 0:
                                    act.wait_ge(kf_used, KF_USED_0 + g)
                                nc.scalar.activation(kf[:, t, :], bk[:, P:2 * P], ACT.Copy).then_inc(kf_ready, 1)
                            nc.scalar.activation(vf[:, tile, :], bk[:, 2 * P:3 * P].rearrange("p (a d) -> p a d", a=1),
                                                 ACT.Copy).then_inc(tok_read, 1)

                groups(act, None, 0, prepare, body)
                if kind == "qkv" and c == 0:
                    act.wait_ge(sd2_var, 1)
                    nc.scalar.activation(sd[:], sd[:], ACT.Sqrt).then_inc(sd2_ready, 1)

            def attention(layer):
                nh = len(halves[layer])

                def exps(hB, c):
                    n2 = cn2(layer, hB, c)
                    act.wait_ge(l_ready, L_READY_0 + n2 + 1)
                    act.wait_ge(pv_done, PV_DONE_0 + n2 - 3)
                    off = first_query(layer, c)
                    nc.scalar.activation(G[:, c % 4, off:512], lbank(layer, c)[:, off:512], ACT.Exp).then_inc(exp_ready, 1)

                def signs(h, c):
                    n2 = cn2(0, h, c)
                    act.wait_ge(z_ready, n2 + 1)
                    act.wait_ge(pv_done, PV_DONE_0 + n2 - 3)
                    nc.scalar.activation(sgn[:, c % 4, :], bank(ZB), ACT.Sign, bias=tiny[:]).then_inc(n_ready, 1)

                def copy_o(hB, qb):
                    k = 2 * ch(layer, hB) + qb
                    act.wait_ge(pv_done, PV_DONE_0 + cn2(layer, hB, nh if qb else TURN[layer]))
                    act.wait_ge(fin_psum, FIN_PSUM_0 + k)
                    nc.scalar.activation(osb[:], bank(OB), ACT.Copy).then_inc(o_copied, 1)

                def count0(h, p, i):
                    n = h * QT_TILES + i
                    if i == 0:
                        act.wait_ge(pst_ready, h + 1)
                    act.wait_ge(s_ready, n + 1)
                    nc.scalar.activation(junk[:, 0, :], SA(i), ACT.Sign, bias=pst[:, p, 0, i:i + 1], scale=-1.0,
                                         accum_out=cs[:, 0, i % 2:i % 2 + 1]).then_inc(c0_done, 1)

                def count1(h, p, i):
                    n = h * QT_TILES + i
                    act.wait_ge(t1_ready, n + 1)
                    nc.scalar.activation(junk[:, 1, :], SA(i), ACT.Sign, bias=t1[:, i % 2:i % 2 + 1], scale=-1.0,
                                         accum_out=cs[:, 1, i % 2:i % 2 + 1]).then_inc(c1_done, 1)

                def step(s, p, has):
                    for i in range(QT_TILES):
                        here = periods[layer][i] if "B" in has else []
                        following = None
                        if layer == 0 and "A" in has and i < QT_TILES - 1:
                            following = (s, p, i + 1)
                        if layer == 0 and "N" in has and i == QT_TILES - 1:
                            following = (s + 1, 1 - p, 0)
                        if layer == 0:
                            for c in here[1:]:
                                signs(s - 2, c)
                        for c in here[:1]:
                            exps(s - 2, c)
                        if i == 0 and "P" in has:
                            copy_o(s - 3, 1)
                        if "B" in has and TURN[layer] in here[:1]:
                            copy_o(s - 2, 0)
                        if following:
                            count0(*following)
                        for c in here[1:]:
                            exps(s - 2, c)
                            if c == TURN[layer]:
                                copy_o(s - 2, 0)
                        if following:
                            count1(*following)
                        if "S" in has and i == TM_PERIOD[layer]:
                            k = ch(layer, s - 1)
                            act.wait_ge(tm_psum, k + 1)
                            act.wait_ge(tm_stored, TM_STORED_0 + 16 * k)
                            nc.scalar.activation(tmT[:], bank(XB)[0:48, 256:320].bitcast(bf), ACT.Copy).then_inc(tm_copied, 1)
                            if layer == 0:
                                act.wait_ge(mx_ready, s)
                                nc.scalar.activation(em[:, 1 - p, :], sm[:, 6 + 1 - p, :], ACT.Exp,
                                                     scale=-1.0).then_inc(em_ready, 1)

                if layer == 0:
                    count0(0, 0, 0)
                    count1(0, 0, 0)
                over_steps(step, lambda: act.Fori(0, LOOPS))

            act.wait_ge(const_in, 16 * 22)
            for s in range(len(STAGES)):
                if s in LN_OF:
                    layer_norm(s)
                stage(s)
                if attention_of(s) is not None:
                    attention(attention_of(s))

        @block.tensor
        def _(pe):
            mm = nc.tensor.matmul

            def stage(s):
                kind, c, xo = STAGES[s]

                def prepare(b, half):
                    gg = 4 * s + b * 2 + half
                    pe.wait_ge(h_ready, gg + 1)
                    pe.wait_ge(hT_ready, HT_READY_0 + gg)
                    for t in range(4):
                        ins = nc.tensor.transpose(bank(XB)[:, t * P:(t + 1) * P], h[:, half, t, :], ident)
                    ins.then_inc(hT_psum, 1)

                def body(b, half):
                    g = b * 2 + half
                    pe.wait_ge(hT_ready, HT_READY_0 + 4 * s + g + 1)
                    rhs = hT[:, half, :]
                    if xo is not None:
                        yy = 4 * xo + g
                        Y = bank(4 + half)
                        pe.wait_ge(x_ready, X_READY_0 + yy - 1)
                    if kind == "ffn":
                        def down(fc):
                            pe.wait_ge(mix_ready, MIX_READY_0 + (c * 4 + g) * FC + fc + 1)
                            for t in range(4):
                                ins = mm(Y[:, t * P:(t + 1) * P], mix[:, fc, t * P:(t + 1) * P], wo_sb[:, fc, :],
                                         start=(fc == 0 and t == 0), stop=(fc == FC - 1), skip_group_check=True)
                            return ins
                        for fc in range(FC):
                            u = (c * 4 + g) * FC + fc
                            for k in range(TOPK):
                                pe.wait_ge((relu0_ready, relu1_ready)[k], RELU0_READY_0 + u - 1)
                                ins = mm(bank(2 * k + fc % 2), wk_ff[:, k, fc * P:(fc + 1) * P], rhs, start=True, stop=True)
                                ins.then_inc(a_psum, 1)
                            if fc:
                                down(fc - 1)
                        down(FC - 1).then_inc(y_psum, 1)
                    if kind == "tern":
                        for t in range(4):
                            ins = mm(Y[:, t * P:(t + 1) * P], hT[:, half, t * P:(t + 1) * P], wtern[:], start=True, stop=True)
                        ins.then_inc(y_psum, 1)
                    if kind == "proj":
                        for t in range(4):
                            mm(Y[:, t * P:(t + 1) * P], ones[0:1, :], brow[0:1, c, 3, :], start=True, stop=False)
                            ins = mm(Y[:, t * P:(t + 1) * P], hT[:, half, t * P:(t + 1) * P], wo_a[:, c, :], start=False, stop=True)
                        ins.then_inc(y_psum, 1)
                    if kind == "qkv":
                        kg = c * 4 + g
                        w = w1 if c else w0
                        for j in range(2):
                            pe.wait_ge(qk_read, QK_READ_0 + 2 * kg + j - 1)
                            ins = mm(bank(j), w[:, j, :], rhs, start=True, stop=True)
                            if c:
                                ins = mm(bank(2 + j), w1s[:, j, :], rhs, start=True, stop=True)
                            ins.then_inc(qk_psum, 1)
                        for t in range(4):
                            pe.wait_ge(tok_read, TOK_READ_0 + kg * 4 + t - 1)
                            lo = 2 if c else 0
                            o = bank(4 + t % 2)[:, lo * P:3 * P]
                            mm(o, ones[0:1, :], brow[0:1, c, lo:3, :], start=True, stop=False)
                            mm(o, hT[:, half, t * P:(t + 1) * P], w[:, lo:3, :], start=False, stop=True).then_inc(tok_psum, 1)
                        if c == 0:
                            pe.wait_ge(kf_ready, 4 * (g + 1))
                            if half == 0:
                                pe.wait_ge(stat_read, STAT_READ_0 + b * QT_TILES)
                            for t in range(4):
                                st, sp_ = half == 0 and t == 0, half == 1 and t == 3
                                mm(bank(6)[:, 0:P], kf[:, t, :], kf[:, t, :], start=st, stop=False, skip_group_check=True)
                                mm(bank(2)[0:1, 0:P], ones[:, 0:1], kf[:, t, :], start=st, stop=sp_)
                                ins = mm(bank(3)[:, 0:1], kf[:, t, :], ones[:, 0:1], start=st, stop=sp_)
                            ins.then_inc(kf_used, 1)
                            if half == 1:
                                pe.wait_ge(cov_row, b + 1)
                                mm(bank(6)[:, 0:P], krow[0:1, 1, :], krow[0:1, 0, :], start=False, stop=True,
                                   skip_group_check=True).then_inc(cov_full, 1)
                                pe.wait_ge(cov_ready, b + 1)
                                pe.wait_ge(qb_ready, 2 * b + 2)
                                for t in range(QT_TILES):
                                    j = b * QT_TILES + t
                                    pe.wait_ge(stat_read, STAT_READ_0 + j - 1)
                                    nc.tensor.matmul(bank(2 + t % 2)[:, 0:144], qb[:, j, :], cov[:],
                                                     start=True, stop=True).then_inc(stat_psum, 1)

                groups(pe, None, 0, prepare, body)

            def attention(layer):
                nh = len(halves[layer])
                wide = WIDE[layer]

                def scores(h, p, i):
                    n = cn(layer, h, i)
                    slot = ch(layer, h) % 4
                    if i == 0:
                        loaded(pe, layer, h, p)
                    pe.wait_ge(s_free, S_FREE_0 + n - 1)
                    width = SEQ if layer == 0 else (i + 1) * P
                    for b2 in range(2):
                        w = min(512, width - 512 * b2)
                        if w > 0:
                            ins = mm(bank(2 * (i % 2) + b2)[:, 0:w], QT[0:CROWS, slot, i * P:(i + 1) * P],
                                     KT[0:CROWS, slot, b2 * 512:b2 * 512 + w], start=True, stop=True)
                    if layer == 1:
                        ins = mm(bank(2 * (i % 2) + i // 4)[:, (i % 4) * P:(i % 4 + 1) * P], negbig[:], upb[:],
                                 start=False, stop=True, skip_group_check=True)
                    ins.then_inc(s_ready, 1)

                def push_down(h, i):
                    pe.wait_ge(ind_ready, h * QT_TILES + i + 1)
                    for b2 in range(2):
                        ins = mm(bank(2 * (i % 2) + b2), negbig[:], ind[:, i % 2, b2 * 512:(b2 + 1) * 512],
                                 start=False, stop=True, skip_group_check=True)
                    ins.then_inc(masked, 1)

                def products(h, p, c0):
                    k = 2 * ch(layer, h) + halves[layer][c0][0]
                    last = 8 if layer == 0 else 4 * halves[layer][c0][0] + 4
                    if halves[layer][c0][1] == 0:
                        pe.wait_ge(o_copied, O_COPIED_0 + k)
                    pe.wait_ge(exp_ready, EXP_READY_0 + cn2(layer, h, c0 + wide))
                    if layer == 0:
                        for c in range(c0, c0 + wide):
                            kt = halves[layer][c][1]
                            q0 = 64 + 32 * (kt % 2)
                            mm(bank(OB)[q0:q0 + 32, :], vu[:, p, kt, :], sgn[:, c % 4, :], start=kt < wide, stop=kt >= last - wide)
                    for c in range(c0, c0 + wide):
                        kt = halves[layer][c][1]
                        q0 = 32 * (kt % wide)
                        off = first_query(layer, c)
                        mm(bank(OB)[q0:q0 + 32, off:512], vg[:, p, kt, :], G[:, c % 4, off:512], start=kt < wide,
                           stop=kt >= last - wide, skip_group_check=True).then_inc(pv_done, 1)

                def final(h, qb):
                    k = 2 * ch(layer, h) + qb
                    pe.wait_ge(o_copied, O_COPIED_0 + k + 1)
                    if qb == 0:
                        pe.wait_ge(fin_done, FIN_DONE_0 + ch(layer, h))
                    w = 18 if layer == 0 else 9
                    cc = C_SEL0 if layer == 0 else C_SEL1
                    for t in range(4):
                        q = qb * 4 + t
                        rows = 32 * (t + 1) if layer and qb == 0 else P
                        ins = mm(bank(XB)[:, q * 18:q * 18 + w], osb[0:rows, t * P:(t + 1) * P], cst[0:rows, cc:cc + w],
                                 start=True, stop=True)
                    ins.then_inc(fin_psum, 1)

                def relative(h, c):
                    kk, qq = halves[0][c][1] * P, halves[0][c][0] * 512
                    if c == 0:
                        pe.wait_ge(tm_loaded, TM_LOADED_0 + 16 * (ch(0, h) + 1))
                    pe.wait_ge(n_ready, N_READY_0 + cn2(0, h, c))
                    mm(bank(ZB), KT[0:ZROWS, h % 4, kk:kk + P], QT[0:ZROWS, h % 4, qq:qq + 512],
                       start=True, stop=True).then_inc(z_ready, 1)

                def shifted(h, c):
                    slot = ch(layer, h) % 4
                    qb, kt = halves[layer][c]
                    n2 = cn2(layer, h, c)
                    L = lbank(layer, c)
                    kk, qq = kt * P, qb * 512
                    if layer == 0:
                        pe.wait_ge(exp_ready, EXP_READY_0 + n2)
                        if c % 2 == 0:
                            mm(L, negbig[:], sgn[:, c % 4, :], start=True, stop=False)
                        else:
                            mm(L, minus[:], onesb[:], start=True, stop=False)
                            mm(L, halfbig[:], sgn[:, c % 4, :], start=False, stop=False)
                        ins = mm(L, KT[0:YROWS, slot, kk:kk + P], QT[0:YROWS, slot, qq:qq + 512], start=False, stop=True)
                    else:
                        if c == 0:
                            pe.wait_ge(tm_loaded, TM_LOADED_0 + 16 * (ch(1, h) + 1))
                        pe.wait_ge(exp_ready, EXP_READY_0 + n2 - 1)
                        off = first_query(1, c)
                        ins = mm(L[:, off:512], KT[0:ZROWS, slot, kk:kk + P], QT[0:ZROWS, slot, qq + off:qq + 512],
                                 start=True, stop=True)
                        if kt >= 4 * qb:
                            ins = mm(L[:, off:off + P], negbig[:], maskb[:], start=False, stop=True, skip_group_check=True)
                    ins.then_inc(l_ready, 1)

                def half_step(s, p, c, has):
                    h = s - 2
                    if layer == 0:
                        pe.wait_ge(n_ready, N_READY_0 + cn2(0, h, c) + 1)
                        if c + 1 < nh:
                            relative(h, c + 1)
                        elif "M" in has:
                            relative(h + 1, 0)
                    shifted(h, c)
                    if c == 0 and "P" in has:
                        products(s - 3, 1 - p, nh - wide)
                    if c == wide:
                        pe.wait_ge(staged, 4 * (h + 1) if layer == 0 else 4 * HB + h + 1)
                    if c and c % wide == 0:
                        products(h, p, c - wide)

                def search(s):
                    h = s - 1
                    pe.wait_ge(bad_int, h + 1)
                    settled(pe)
                    bad = pe.value_load(badi[0:1, QT_TILES:], min_val=0, max_val=P * QT_TILES)
                    with pe.If(bad > 0):
                        with pe.Fori(0, QT_TILES) as t:
                            pe.wait_ge(fb_read, FB_READ_0 + 2 * (h * QT_TILES + t))
                            settled(pe)
                            bad_tile = pe.value_load(badi[0:1, bass.ds(t, 1)], min_val=0, max_val=P)
                            with pe.If(bad_tile > 0):
                                for b2 in range(2):
                                    if b2:
                                        pe.wait_ge(fb_read, FB_READ_0 + 2 * (h * QT_TILES + t) + 1)
                                    mm(bank(XB), QT[0:CROWS, h % 4, bass.ds(t * P, P)],
                                       KT[0:CROWS, h % 4, b2 * 512:(b2 + 1) * 512], start=True, stop=True).then_inc(fb_s, 1)
                            with pe.Else():
                                pe.sem_inc(fb_s, 2)
                    with pe.Else():
                        pe.sem_inc(fb_s, 2 * QT_TILES)

                def step(s, p, has):
                    for i in range(QT_TILES):
                        here = periods[layer][i] if "B" in has else []
                        if layer == 0 and i == 0 and "S" in has:
                            push_down(s - 1, QT_TILES - 1)
                        if layer == 0 and i and "A" in has:
                            push_down(s, i - 1)
                        for c in here[:1]:
                            half_step(s, p, c, has)
                        if i == 0 and has == "P":
                            products(s - 3, 1 - p, nh - wide)
                        if i < QT_TILES - 1 and "A" in has:
                            scores(s, p, i + 1)
                        if i == QT_TILES - 1 and "N" in has:
                            scores(s + 1, 1 - p, 0)
                        if i == 1 and "P" in has:
                            final(s - 3, 1)
                        if layer == 0 and "S" in has and i == 4:
                            search(s)
                        if "S" in has and i == TM_PERIOD[layer]:
                            pe.wait_ge(tm_ready, ch(layer, s - 1) + 1)
                            if "P" in has:
                                pe.wait_ge(fin_done, FIN_DONE_0 + ch(layer, s - 3) + 1)
                            settled(pe)
                            nc.tensor.transpose(bank(XB)[0:48, 256:320].bitcast(bf), tmp[:].rearrange("p t w r -> p (t w r)"),
                                                identb[:]).then_inc(tm_psum, 1)
                        if i == 6 and "B" in has:
                            if "S" in has:
                                pe.wait_ge(tm_copied, ch(layer, s - 1) + 1)
                            final(s - 2, 0)
                        for c in here[1:]:
                            half_step(s, p, c, has)
                        if layer == 0 and "S" in has and i == 3:
                            pe.wait_ge(bad_ready, BAD_READY_0 + s)
                            mm(bank(XB)[0:1, 256:256 + QT_TILES + 1], ones[:, 0:1], badt[:], start=True, stop=True).then_inc(bad_psum, 1)
                        if layer == 0 and i == QT_TILES - 1 and "M" in has and "B" not in has:
                            relative(s - 1, 0)

                pe.wait_ge(qk_read, QK_READ_0 + 8 * (layer + 1))
                pe.wait_ge(tok_read, TOK_READ_0 + TILES * (layer + 1))
                pe.wait_ge(stat_read, STAT_READ_0 + TILES)
                if layer == 0:
                    pe.wait_ge(hT_ready, HT_READY_0 + 8)
                    for b in range(BATCH):
                        for t in range(1, QT_TILES, 2):
                            ins = mm(bank(XB)[:, b * HID:(b + 1) * HID], ones[:], vf[:, b * QT_TILES + t, :],
                                     start=t == 1, stop=t == QT_TILES - 1)
                    ins.then_inc(vsum_psum, 1)
                scores(0, 0, 0)
                over_steps(step, lambda: pe.Fori(0, LOOPS))

            pe.wait_ge(prep_done, 1)
            for k in range(TOPK):
                for fc in range(FC):
                    mm(bank(k)[:, fc * P:(fc + 1) * P], wi_sb[:, fc * P:(fc + 1) * P], ident, start=True, stop=False)
                    ins = mm(bank(k)[:, fc * P:(fc + 1) * P], la[:], lbs[:, k, fc * P:(fc + 1) * P], start=False, stop=True)
            ins.then_inc(ffw_psum, 1)
            mm(bank(2)[:, 0:1], ones[:], wabs[:], start=True, stop=True).then_inc(tern_psum, 1)
            pe.wait_ge(ffw_done, 2)
            for s in range(len(STAGES)):
                stage(s)
                if attention_of(s) is not None:
                    attention(attention_of(s))

        @block.vector
        def _(dve):
            V = nc.vector
            seq = Seq(dve, dve_seq)
            link = seq.link

            dve.wait_ge(const_in, 16 * 22)
            link(V.tensor_copy(identb[:], ident))
            link(V.tensor_scalar(negbig[:], ident, -BIG, None, ALU.mult))
            link(V.tensor_copy(upb[:], cst[:, C_UP:C_UP + P]))
            link(V.tensor_copy(maskb[:], cst[:, C_MASK:C_MASK + P]))
            link(V.memset(ones[:], 1.0))
            link(V.memset(eps[:], EPS))
            link(V.tensor_scalar(halfbig[:], ident, BIG / 2, None, ALU.mult))
            link(V.memset(minus[:], -BIG / 2))
            link(V.memset(onesb[:], 1.0))
            link(V.memset(tiny[:], 1e-30))
            link(V.memset(vhalf[:], SEQ / 4))
            link(V.memset(KT[:], 1.0))
            link(V.memset(QT[:], 0.0))
            link(V.memset(vg[:], 0.0))
            link(V.memset(vg[:, :, :, HD:HD + 1], 1.0))
            link(V.memset(vu[:], 0.0))
            link(V.memset(vu[:, :, :, 3 * HD:3 * HD + 1], 1.0))
            link(V.memset(tm[:], 0.0))
            link(V.tensor_copy(idxf[:], idx_sb[:]))
            for k in range(TOPK):
                link(V.tensor_scalar(esel[:, k:k + 1], idxf[:, k:k + 1], cst[:, C_EXP:C_EXP + 1], None, ALU.is_equal))
                link(V.tensor_scalar(lbs[:, k, :], lb[:], esel[:, k:k + 1], None, ALU.mult))
            link(V.tensor_reduce(wabs[:], wt_sb[:], AX.X, ALU.add, apply_absolute_value=True))
            link(V.memset(mark[:], 0.0))
            V.memset(mark[:], 0.0).then_inc(prep_done, 1)
            dve.wait_ge(ffw_psum, 1)
            V.tensor_copy(wk_ff[:], ps[:, 0:2, :]).then_inc(ffw_done, 1)
            dve.wait_ge(tern_psum, 1)
            link(V.tensor_scalar(wscale[:, 0:1], bank(2)[:, 0:1], 1.0 / (P * P), EPS, ALU.mult, ALU.max))
            link(V.tensor_scalar(wscale[:, 1:2], wscale[:, 0:1], 0.5, None, ALU.mult))
            link(V.tensor_scalar(wscale[:, 2:3], wscale[:, 0:1], -0.5, None, ALU.mult))
            link(V.tensor_scalar(wneg[:], wt_sb[:], wscale[:, 2:3], None, ALU.is_lt))
            link(V.scalar_tensor_tensor(wtern[:], wt_sb[:], wscale[:, 1:2], wneg[:], ALU.is_gt, ALU.subtract))
            V.tensor_scalar(wtern[:], wtern[:], wscale[:, 0:1], None, ALU.mult).then_inc(ffw_done, 1)
            dve.wait_ge(x_in_done, 16)

            LINKS_STEPS = {0: 554, 1: 14}
            LINKS = {("ffn", 0): 0, ("ffn", 1): 0, ("proj", 0): 0, ("proj", 1): 0, ("tern", 0): 0, ("tern", 1): 0,
                     ("qkv", 0): 35, ("qkv", 1): 26}

            def layer_norm(s):
                n = LN_OF[s]
                if X_BEFORE[s]:
                    dve.wait_ge(x_ready, X_READY_0 + 4 * X_BEFORE[s])
                with seq.loop(4, 4) as g:
                    for t in range(4):
                        link(V.bn_stats(stat[:, bass.ds(g * 4 + t, 1), :], x[:, bass.ds(g * 4 + t, 1), :]))
                me, m2e, mo, m2o = (stat[:, :, j] for j in (1, 2, 4, 5))
                link(V.tensor_tensor(ln[:, 0, :], me, mo, ALU.add))
                link(V.tensor_tensor(ln[:, 3, :], me, mo, ALU.subtract))
                link(V.tensor_tensor(ln[:, 1, :], m2e, m2o, ALU.add))
                link(V.tensor_tensor(ln[:, 3, :], ln[:, 3, :], ln[:, 3, :], ALU.mult))
                link(V.tensor_scalar(ln[:, 1, :], ln[:, 1, :], 1.0 / HID, None, ALU.mult))
                V.scalar_tensor_tensor(ln[:, 1, :], ln[:, 3, :], 0.25, ln[:, 1, :], ALU.mult, ALU.add).then_inc(var_ready, 1)
                dve.wait_ge(sd_ready, n + 1)
                link(V.reciprocal(ln[:, 4, :], ln[:, 2, :]))
                link(V.scalar_tensor_tensor(ln[:, 5, :], ln[:, 0, :], -0.5, ln[:, 4, :], ALU.mult, ALU.mult))

            def stage(s):
                kind, c, xo = STAGES[s]

                def make_h(g, half):
                    gg = 4 * s + g
                    dve.wait_ge(hT_ready, HT_READY_0 + gg - 1)
                    for t in range(4):
                        tile = bass.ds(g * 4 + t, 1)
                        o = h[:, half, t, :].rearrange("p (a d) -> p a d", a=1)
                        if kind == "proj":
                            ins = V.tensor_copy(o, ao[:, tile, :])
                        else:
                            ins = V.tensor_scalar(o, x[:, tile, :], ln[:, 4, tile], ln[:, 5, tile], ALU.mult, ALU.add)
                    ins.then_inc(h_ready, 1)

                def split(w):
                    a = qk_t[:, w, :]
                    r = res1[:, w, :]
                    link(V.tensor_copy(parts[:, w, 0, :], a))
                    link(V.tensor_tensor(r, a, parts[:, w, 0, :], ALU.subtract))
                    link(V.tensor_copy(parts[:, w, 1, :], r))
                    link(V.tensor_tensor(r, r, parts[:, w, 1, :], ALU.subtract))
                    V.tensor_copy(parts[:, w, 2, :], r).then_inc(part_ready, 1)

                def prepare(b, half):
                    make_h(b * 2 + half, half)

                def body(b, half):
                    g = b * 2 + half
                    if xo is not None:
                        yy = 4 * xo + g
                    if kind == "ffn":
                        for fc in range(FC):
                            u = (c * 4 + g) * FC + fc
                            dve.wait_ge(a_psum, 2 * u + 2)
                            V.tensor_scalar(relu1[:, fc % 2, :], bank(2 + fc % 2), 0.0, val_sb[:, 1:2], ALU.max,
                                            ALU.mult).then_inc(relu1_ready, 1)
                            dve.wait_ge(relu1_ready, RELU1_READY_0 + u + 1)
                            dve.wait_ge(relu0_ready, RELU0_READY_0 + u + 1)
                            dve.wait_ge(y_psum, Y_PSUM_0 + yy)
                            V.scalar_tensor_tensor(mix[:, fc, :], relu0[:, fc % 2, :], val_sb[:, 0:1], relu1[:, fc % 2, :],
                                                   ALU.mult, ALU.add).then_inc(mix_ready, 1)
                    if xo is not None:
                        dve.wait_ge(y_psum, Y_PSUM_0 + yy + 1)
                        xt = x[:, bass.ds(g * 4, 4), :]
                        V.scalar_tensor_tensor(xt, bank(4 + half).rearrange("p (a d) -> p a d", a=4),
                                               1.0 if kind == "proj" else 0.5, xt, ALU.mult, ALU.add).then_inc(x_ready, 1)
                    if kind == "qkv":
                        kg = c * 4 + g
                        dve.wait_ge(part_stored, PART_STORED_0 + 32 * kg)
                        for w in range(2):
                            dve.wait_ge(qk_psum, 2 * kg + w + 1)
                            if c == 0:
                                V.tensor_scalar(qk_t[:, w, :], bank(w), bcol[:, w:w + 1], ISQ if w == 0 else 1.0,
                                                ALU.add, ALU.mult).then_inc(qk_read, 1)
                                dve.wait_ge(qk_read, QK_READ_0 + 2 * kg + w + 1)
                            else:
                                cos = cst[:, C_ROPE + half * 512:C_ROPE + half * 512 + 512]
                                sin = cst[:, C_ROPE + SEQ + half * 512:C_ROPE + SEQ + half * 512 + 512]
                                link(V.scalar_tensor_tensor(qk_t[:, w, :], bank(w), bcol[:, 2 + w:3 + w], cos, ALU.add, ALU.mult))
                                V.scalar_tensor_tensor(rot[:, w, :], bank(2 + w), bcol[:, 4 + w:5 + w], sin, ALU.add,
                                                       ALU.mult).then_inc(qk_read, 1)
                                dve.wait_ge(qk_read, QK_READ_0 + 2 * kg + w + 1)
                                link(V.tensor_tensor(qk_t[:, w, :], qk_t[:, w, :], rot[:, w, :], ALU.add))
                                if w == 0:
                                    link(V.tensor_scalar(qk_t[:, w, :], qk_t[:, w, :], ISQ, None, ALU.mult))
                            split(w)
                            if c == 0 and w == 0:
                                V.tensor_copy(qb[:, bass.ds(g * 4, 4), :],
                                              parts[:, 0, 0, :].rearrange("p (a d) -> p a d", a=4)).then_inc(qb_ready, 1)
                        if c == 0 and half == 1:
                            dve.wait_ge(kf_used, KF_USED_0 + g + 1)
                            link(V.tensor_copy(krow[0:1, 0, :], bank(2)[0:1, 0:P]))
                            link(V.tensor_copy(kcol[:], bank(3)[:, 0:1]))
                            V.tensor_scalar(krow[0:1, 1, :], krow[0:1, 0, :], -1.0 / SEQ, None, ALU.mult).then_inc(cov_row, 1)
                            dve.wait_ge(cov_full, b + 1)
                            link(V.tensor_tensor(cov[:, 0:P], bank(6)[:, 0:P], cst[:, C_HEAD:C_HEAD + P], ALU.mult))
                            V.tensor_scalar(cov[:, P:P + HEADS], cst[:, C_HSEL:C_HSEL + HEADS], kcol[:], None,
                                            ALU.mult).then_inc(cov_ready, 1)
                            for t in range(QT_TILES):
                                j = b * QT_TILES + t
                                bk = bank(2 + t % 2)
                                tile = bass.ds(j, 1)
                                dve.wait_ge(stat_psum, j + 1)
                                link(V.tensor_tensor(qc[:].rearrange("p (a d) -> p a d", a=1),
                                                     bk[:, 0:P].rearrange("p (a d) -> p a d", a=1), qtok[:, tile, :], ALU.mult))
                                V.tensor_copy(mu[:, tile, :], bk[:, P:P + HEADS].rearrange("p (a d) -> p a d", a=1)).then_inc(stat_read, 1)
                                link(V.tensor_reduce(sd[:, tile, :].rearrange("p a d -> p (a d)"), qc[:].rearrange("p (h d) -> p h d", d=HD), AX.X, ALU.add))

                groups(dve, seq, LINKS[kind, c], prepare, body)
                if kind == "qkv":
                    dve.wait_ge(tok_read, TOK_READ_0 + 16 * (c + 1))
                    if c == 0:
                        V.tensor_scalar(sd[:], sd[:], 1e-12, None, ALU.max).then_inc(sd2_var, 1)
                        dve.wait_ge(stat_read, STAT_READ_0 + TILES)
                        dve.wait_ge(sd2_ready, 1)
                        link(V.scalar_tensor_tensor(par[:, 0], sd[:], Z_START, mu[:], ALU.mult, ALU.add))
                        link(V.tensor_scalar(par[:, 1], sd[:], -0.5 / DENSITY1, None, ALU.mult))
                        link(V.tensor_scalar(par[:, 4], sd[:], -0.5 / DENSITY2, None, ALU.mult))
                        link(V.scalar_tensor_tensor(par[:, 2], sd[:], (SEQ / 2 - AIM1) / DENSITY1, par[:, 0], ALU.mult, ALU.add))
                        V.scalar_tensor_tensor(par[:, 3], sd[:], (SEQ / 2 - AIM2) / DENSITY2, par[:, 2], ALU.mult,
                                               ALU.add).then_inc(par_ready, 1)
                        link(V.tensor_copy(vp[:, 0], vf[:]))
                        link(V.tensor_tensor(vres[:], vf[:], vp[:, 0], ALU.subtract))
                        link(V.tensor_copy(vp[:, 1], vres[:]))
                        link(V.tensor_tensor(vres[:], vres[:], vp[:, 1], ALU.subtract))
                        link(V.tensor_copy(vp[:, 2], vres[:]))
                        dve.wait_ge(vsum_psum, 1)
                        link(V.tensor_scalar(vhalf[:, :, 0:HD], bank(XB)[:, 0:BATCH * HID].rearrange("p (h d) -> p h d", d=HD),
                                             0.5, None, ALU.mult))
                    V.memset(mark[:], 0.0).then_inc(v_ready, 1)

            def attention(layer):
                def below(h, c):
                    n2 = cn2(0, h, c)
                    dve.wait_ge(z_ready, n2 + 1)
                    dve.wait_ge(pv_done, PV_DONE_0 + n2 - 3)
                    V.tensor_scalar(sgn[:, c % 4, :], bank(ZB), 0.0, None, ALU.is_lt).then_inc(n_ready, 1)

                def largest(h, p, i, half):
                    n = h * QT_TILES + i
                    if half == 0:
                        dve.wait_ge(masked, n + 1)
                        settled(dve)
                    w = SEQ // SEGS
                    for sg in range(half * SEGS // 2, (half + 1) * SEGS // 2):
                        ins = V.max(cand[:, p, i, sg * 8:sg * 8 + 8], SA(i)[:, sg * w:(sg + 1) * w])
                    if half == 1:
                        ins.then_inc(s_free, 1)

                def sort(h, p, i, k):
                    lists = (cand[:, p, i, :], cand2[:, 0, :], cand2[:, 1, :])
                    if k == 0:
                        dve.wait_ge(s_free, S_FREE_0 + h * QT_TILES + i + 1)
                    else:
                        dve.wait_ge(dve_seq, written["sort"])
                    settled(dve)
                    eight = srt[:, p, i, 1 + 8 * (k // 2):9 + 8 * (k // 2)]
                    if k % 2 == 0:
                        ins = V.max(eight, lists[k // 2])
                    else:
                        ins = V.match_replace(lists[k // 2 + 1], eight, lists[k // 2], LOWEST)
                    seq.count(ins)
                    written["sort"] = seq.n

                written = {}
                at, thr, lm, ok = (sm[:, j, :] for j in range(4))

                def select(h, p, k):
                    shape = [P, QT_TILES, NSORT + 1]
                    it = cst[:, C_IOTA:C_IOTA + NSORT + 1].rearrange("p (a n) -> p a n", a=1).to_broadcast(shape)
                    if k == 0:
                        dve.wait_ge(dve_seq, seq.n)
                        seq.count(V.tensor_scalar(at, cnt[:, p, :], -1.0, KEEP + 0.5, ALU.mult, ALU.add))
                        seq.count(V.tensor_reduce(lm, cand[:, p].rearrange("p t (s e) -> p t s e", e=8)[:, :, :, 7], AX.X, ALU.max))
                    if k == 1:
                        dve.wait_ge(dve_seq, seq.n)
                        seq.count(V.tensor_tensor(sel[:], it, at.rearrange("p (t a) -> p t a", a=1).to_broadcast(shape), ALU.subtract))
                        seq.count(V.tensor_scalar(ok, at, NSORT - 0.4, None, ALU.is_le))
                    if k == 2:
                        dve.wait_ge(dve_seq, seq.n)
                        seq.count(V.tensor_tensor(sel[:], sel[:], sel[:], ALU.mult))
                        seq.count(V.scalar_tensor_tensor(ok, at, 0.4, ok, ALU.is_ge, ALU.mult))
                    if k == 3:
                        dve.wait_ge(dve_seq, seq.n)
                        seq.count(V.scalar_tensor_tensor(sel[:], sel[:], 1.0, srt[:, p], ALU.is_lt, ALU.mult))
                    if k == 4:
                        dve.wait_ge(dve_seq, seq.n)
                        seq.count(V.tensor_reduce(thr, sel[:], AX.X, ALU.add))
                    if k == 5:
                        dve.wait_ge(dve_seq, seq.n)
                        seq.count(V.scalar_tensor_tensor(lm, thr, 0.5, lm, ALU.mult, ALU.is_gt))
                    if k == 6:
                        dve.wait_ge(dve_seq, seq.n)
                        seq.count(V.tensor_tensor(ok, ok, lm, ALU.mult))
                    if k == 7:
                        dve.wait_ge(dve_seq, seq.n)
                        seq.count(V.tensor_scalar(badt[:, 0:QT_TILES], ok, -1.0, 1.0, ALU.mult, ALU.add))
                    if k == 8:
                        dve.wait_ge(dve_seq, seq.n)
                        V.tensor_reduce(badt[:, QT_TILES:], badt[:, 0:QT_TILES], AX.X, ALU.add).then_inc(bad_ready, 1)

                def search(h):
                    dve.wait_ge(bad_int, h + 1)
                    settled(dve)
                    bad = dve.value_load(badi[0:1, QT_TILES:], min_val=0, max_val=P * QT_TILES)
                    rounds, r = KEEP // 8, KEEP % 8
                    per = 1 + 2 * rounds + 2
                    with dve.If(bad > 0):
                        with seq.loop(QT_TILES, per) as t:
                            bad_tile = dve.value_load(badi[0:1, bass.ds(t, 1)], min_val=0, max_val=P)
                            with dve.If(bad_tile > 0):
                                for b2 in range(2):
                                    dve.wait_ge(fb_s, 2 * (h * QT_TILES + t) + b2 + 1)
                                    V.tensor_copy(fw[:, b2 * 512:(b2 + 1) * 512], bank(XB)).then_inc(fb_read, 1)
                                dve.wait_ge(fb_read, FB_READ_0 + 2 * (h * QT_TILES + t) + 2)
                                link(V.memset(fm[:], 0.0), plain=True)
                                with seq.loop(rounds, 2):
                                    link(V.max(fm[:], fw[:]), plain=True)
                                    link(V.match_replace(fw[:], fm[:], fw[:], LOWEST), plain=True)
                                link(V.max(fm[:], fw[:]))
                                link(V.tensor_tensor(sm[:, 1, bass.ds(t, 1)], fm[:, r - 1:r], fm[:, r:r + 1], ALU.add), plain=True)
                            with dve.Else():
                                dve.sem_inc(fb_read, 2)
                                dve.sem_inc(dve_seq, per)
                    with dve.Else():
                        dve.sem_inc(fb_read, 2 * QT_TILES)
                        dve.sem_inc(dve_seq, QT_TILES * per)

                def rows(h, p):
                    if layer == 0:
                        seq.count(V.tensor_scalar(tm[:, :, 0], thr, -0.5, None, ALU.mult))
                        V.tensor_scalar(sm[:, 6 + p, :], rmax[:, p, :], 0.0, None, ALU.max).then_inc(mx_ready, 1)
                        dve.wait_ge(mx_ready, h + 1)
                        link(V.scalar_tensor_tensor(tm[:, :, 1], thr, 0.5, sm[:, 6 + p, :], ALU.mult, ALU.subtract))
                    else:
                        dve.wait_ge(s_free, S_FREE_0 + cn(1, h + 1, 0))
                        link(V.tensor_scalar(tm[:, :, 0], rmax[:, p, :], -1.0, None, ALU.mult))

                def split_rows(k):
                    if k == 0:
                        link(V.tensor_copy(tmp[:, :, :, 0], tm[:]))
                        link(V.tensor_tensor(tmr[:, 0], tm[:], tmp[:, :, :, 0], ALU.subtract))
                    if k == 1:
                        link(V.tensor_copy(tmp[:, :, :, 1], tmr[:, 0]))
                        link(V.tensor_tensor(tmr[:, 1], tmr[:, 0], tmp[:, :, :, 1], ALU.subtract))
                        V.tensor_copy(tmp[:, :, :, 2], tmr[:, 1]).then_inc(tm_ready, 1)

                def finish(h, p):
                    n = ch(layer, h)
                    dve.wait_ge(fin_psum, FIN_PSUM_0 + 2 * (n + 1))
                    fp = bank(XB)[:, 0:144].rearrange("p (t c) -> p t c", c=18)
                    if layer == 0:
                        dve.wait_ge(em_ready, h + 1)
                        link(V.tensor_tensor(fin[:, 0], fp[:, :, 9:18],
                                             vhalf[:, bass.ds(h, 1), :].to_broadcast([P, QT_TILES, 9]), ALU.add))
                        link(V.tensor_tensor(fin[:, 0], fin[:, 0],
                                             em[:, p, :].rearrange("p (t a) -> p t a", a=1).to_broadcast([P, QT_TILES, 9]), ALU.mult))
                        ins = V.tensor_tensor(fin[:, 1], fp[:, :, 0:9], fin[:, 0], ALU.add)
                    else:
                        ins = V.tensor_copy(fin[:, 1], fp[:, :, 0:9])
                    ins.then_inc(fin_done, 1)
                    dve.wait_ge(fin_done, FIN_DONE_0 + n + 1)
                    link(V.reciprocal(frec[:], fin[:, 1, :, 8]))
                    b, hd = h // HEADS, h % HEADS
                    link(V.tensor_tensor(ao[:, bass.ds(b * QT_TILES, QT_TILES), bass.ds(hd * HD, HD)], fin[:, 1, :, 0:HD],
                                         frec[:].rearrange("p (t a) -> p t a", a=1).to_broadcast([P, QT_TILES, HD]), ALU.mult))

                def step(s, p, has):
                    for i in range(QT_TILES):
                        seg = srtd = None
                        if layer == 0:
                            if i >= 1 and "A" in has:
                                seg = (s, p, i - 1)
                            if i == 0 and "S" in has:
                                seg = (s - 1, 1 - p, QT_TILES - 1)
                            if i >= 2 and "A" in has:
                                srtd = (s, p, i - 2)
                            if i < 2 and "S" in has:
                                srtd = (s - 1, 1 - p, QT_TILES - 2 + i)
                        chosen = (s - 1, 1 - p) if layer == 0 and "S" in has and i in (2, 3) else None
                        if layer == 0 and "S" in has and i == 4:
                            dve.wait_ge(bad_psum, s)
                            V.tensor_copy(badi[:], bank(XB)[0:1, 256:256 + QT_TILES + 1]).then_inc(bad_int, 1)
                        if srtd:
                            sort(*srtd, 0)
                        if layer == 0 and "B" in has:
                            below(s - 2, periods[0][i][0])
                        if chosen:
                            select(*chosen, 0 if i == 2 else 5)
                        if srtd:
                            sort(*srtd, 1)
                        if seg:
                            largest(*seg, 0)
                        if chosen:
                            select(*chosen, 1 if i == 2 else 6)
                        if srtd:
                            sort(*srtd, 2)
                        if seg:
                            largest(*seg, 1)
                        if chosen:
                            select(*chosen, 2 if i == 2 else 7)
                        if srtd:
                            sort(*srtd, 3)
                        if chosen:
                            select(*chosen, 3 if i == 2 else 8)
                        if srtd:
                            sort(*srtd, 4)
                        if "A" in has:
                            n = cn(layer, s, i)
                            if layer == 0:
                                dve.wait_ge(c1_done, n + 1)
                            dve.wait_ge(s_ready, n + 1)
                            width = SEQ if layer == 0 else (i + 1) * P
                            ins = V.tensor_reduce(rmax[:, p, i:i + 1], SA(i)[:, 0:width], AX.X, ALU.max)
                            if layer == 1:
                                ins.then_inc(s_free, 1)
                        if layer == 0 and "A" in has:
                            dve.wait_ge(t2_ready, n + 1)
                            V.tensor_scalar(ind[:, i % 2, :], SA(i), srt[:, p, i, 0:1], None, ALU.is_ge, ALU.add,
                                            accum_out=cnt[:, p, i:i + 1]).then_inc(ind_ready, 1)
                        if chosen and i == 2:
                            select(*chosen, 4)
                        if i == 2 and "P" in has:
                            finish(s - 3, 1 - p)
                        if layer == 0 and "S" in has:
                            if i == 4:
                                search(s - 1)
                                rows(s - 1, 1 - p)
                                split_rows(0)
                                split_rows(1)
                        if layer == 1 and "S" in has and i == 0:
                            rows(s - 1, 1 - p)
                            split_rows(0)
                            split_rows(1)

                over_steps(step, lambda: seq.loop(LOOPS, LINKS_STEPS[layer]))

            for s in range(len(STAGES)):
                if s in LN_OF:
                    layer_norm(s)
                stage(s)
                if attention_of(s) is not None:
                    attention(attention_of(s))


def kernel(**inputs):
    import concourse.bacc as bacc
    from concourse.bass_utils import run_bass_kernel_spmd as run

    a = {k: np.asarray(v) for k, v in inputs.items()}
    swap = np.arange(HID) ^ 1
    l0, l1 = "L0_attn_", "L1_attn_"
    host = {
        "consts": shape_constants(),
        "x_in": a["L0_attn_x"].reshape(BATCH * SEQ, HID),
        "wq0": a[l0 + "Wq"], "wk0": a[l0 + "Wk"], "wv0": a[l0 + "Wv"], "wo0": a[l0 + "Wo"],
        "rows0": np.stack([a[l0 + "b" + c] for c in "qkvo"])[None],
        "cols0": np.stack([a[l0 + "b" + c] for c in "qk"], 1),
        "wi": a["L0_ffn_wi_w"].reshape(FC, P, HID).transpose(1, 0, 2).reshape(P, FF),
        "wo_ff": a["L0_ffn_wo_w"].T.reshape(FC, P, HID).transpose(1, 0, 2),
        "lora_a": a["L0_ffn_lora_As"].reshape(EXPERTS * RANK, HID),
        "lora_b": a["L0_ffn_lora_Bs"].transpose(0, 2, 1).reshape(EXPERTS * RANK, FF),
        "idx": np.broadcast_to(a["L0_ffn_top_k_indices"], (P, TOPK)),
        "val": np.broadcast_to(a["L0_ffn_top_k_values"], (P, TOPK)),
        "wq1": a[l1 + "Wq"], "wk1": a[l1 + "Wk"], "wv1": a[l1 + "Wv"], "wo1": a[l1 + "Wp"],
        "rows1": np.stack([a[l1 + "b" + c] for c in "qkvp"])[None],
        "cols1": np.stack([a[l1 + "bq"], a[l1 + "bk"], a[l1 + "bq"][swap], a[l1 + "bk"][swap]], 1),
        "wq1s": a[l1 + "Wq"][:, swap], "wk1s": a[l1 + "Wk"][:, swap],
        "wt": a["L1_ffn_weight"].T,
    }
    nc = bacc.Bacc("TRN2", target_bir_lowering=False, num_devices=1)
    arrays, args = {}, {}
    for name, v in host.items():
        v = np.ascontiguousarray(v)
        arrays["in_" + name] = v
        args[name] = nc.dram_tensor("in_" + name, v.shape, mybir.dt.from_np(v.dtype), kind="ExternalInput").ap()
    for name in ("qs", "ks"):
        args[name] = nc.dram_tensor(name, (BATCH, 3, HID, SEQ), mybir.dt.bfloat16, kind="Internal").ap()
    args["tms"] = nc.dram_tensor("tms", (YROWS - CROWS, SEQ), mybir.dt.bfloat16, kind="Internal").ap()
    args["out"] = nc.dram_tensor("out_x", (BATCH * SEQ, HID), mybir.dt.float32, kind="ExternalOutput").ap()
    macaron_kernel(nc, **args)
    r = run(nc, [arrays], core_ids=[0])
    return r.results[0]["out_x"].reshape(BATCH, SEQ, HID)
```
